# Optimizing a Trainium2 kernel written in Bass

```python
import numpy as np
import jax
import jax.numpy as jnp

def _softmax(x, axis=-1):
    return jax.nn.softmax(x, axis=axis)

def _gelu(x):
    return jax.nn.gelu(x, approximate=True)

def _silu(x):
    return jax.nn.silu(x)

def _sigmoid(x):
    return jax.nn.sigmoid(x)

def _layernorm(x, axis=-1, eps=1e-05):
    m = jnp.mean(x, axis=axis, keepdims=True)
    v = jnp.var(x, axis=axis, keepdims=True)
    return (x - m) / jnp.sqrt(v + eps)

def _scatter_add(tgt, idx, src, axis=0):
    return tgt.at[idx].add(src)

def _segment_sum(src, seg, n):
    return jax.ops.segment_sum(src, seg, n)
kernel_name = 'mk_sandwich_d2_jaxref_r8_1c01ee'

def setup_inputs(seed: int=0):
    np.random.seed(seed)
    _w = jnp.asarray

    def _L0_attn_setup():
        import jax, jax.numpy as jnp
        import numpy as np
        DIM = 256
        D_STATE = 128
        EXPAND = 2
        HEADDIM = 64
        CHUNK = 64
        NGROUPS = 1
        D_INNER = EXPAND * DIM
        NHEADS = D_INNER // HEADDIM
        D_PROJ = D_INNER * 2 + NGROUPS * D_STATE * 2 + NHEADS
        BATCH, SEQ = (2, 512)
        EPS = 1e-05

        def segsum(x):
            T = x.shape[-1]
            xx = jnp.broadcast_to(x[..., :, None], x.shape + (T,))
            keep = jnp.tril(jnp.ones((T, T), dtype=bool), -1)
            xx = jnp.where(keep, xx, 0.0)
            s = jnp.cumsum(xx, axis=-2)
            tri = jnp.tril(jnp.ones((T, T), dtype=bool), 0)
            return jnp.where(tri, s, -jnp.inf)

        def rms_norm(x, w):
            return x * jax.lax.rsqrt(jnp.mean(x * x, axis=-1, keepdims=True) + EPS) * w

        def layer_norm(x, w, b):
            mu = jnp.mean(x, axis=-1, keepdims=True)
            var = jnp.mean((x - mu) ** 2, axis=-1, keepdims=True)
            return (x - mu) * jax.lax.rsqrt(var + EPS) * w + b

        def ssd_chunked(x, A, B, C, chunk):
            b, s, h, p = x.shape
            n = B.shape[-1]
            if B.shape[2] < h:
                r = h // B.shape[2]
                B = jnp.repeat(B, r, axis=2)
                C = jnp.repeat(C, r, axis=2)
            c = s // chunk
            x = x.reshape(b, c, chunk, h, p)
            A = A.reshape(b, c, chunk, h).transpose(0, 3, 1, 2)
            B = B.reshape(b, c, chunk, h, n)
            C = C.reshape(b, c, chunk, h, n)
            L = jnp.exp(segsum(A))
            Y_diag = jnp.einsum('bclhn,bcshn,bhcls,bcshp->bclhp', C, B, L, x)
            A_cumsum = jnp.cumsum(A, axis=-1)
            decay_states = jnp.exp(A_cumsum[..., -1:] - A_cumsum)
            states = jnp.einsum('bclhn,bhcl,bclhp->bchpn', B, decay_states, x)
            A_chunk = jnp.pad(A_cumsum[..., -1], ((0, 0), (0, 0), (1, 0)))
            decay_chunk = jnp.exp(segsum(A_chunk))
            new_states = jnp.einsum('bhzc,bchpn->bzhpn', decay_chunk[:, :, :c, 1:c + 1], states)
            Y_off = jnp.einsum('bclhn,bchpn,bhcl->bclhp', C, new_states, jnp.exp(A_cumsum))
            return (Y_diag + Y_off).reshape(b, s, h, p)

        def mamba3_forward(u, in_proj_w, out_proj_w, D, dt_bias, A_log, bnorm_w, cnorm_w, ln_w, ln_b):
            b, s, _ = u.shape
            u_n = layer_norm(u, ln_w, ln_b)
            proj = jnp.einsum('bsd,ed->bse', u_n, in_proj_w)
            z = proj[..., :D_INNER]
            x = proj[..., D_INNER:2 * D_INNER]
            B = proj[..., 2 * D_INNER:2 * D_INNER + NGROUPS * D_STATE].reshape(b, s, NGROUPS, D_STATE)
            C = proj[..., 2 * D_INNER + NGROUPS * D_STATE:2 * D_INNER + 2 * NGROUPS * D_STATE].reshape(b, s, NGROUPS, D_STATE)
            dt = proj[..., -NHEADS:]
            B = rms_norm(B, bnorm_w)
            C = rms_norm(C, cnorm_w)
            x = x.reshape(b, s, NHEADS, HEADDIM)
            z = z.reshape(b, s, NHEADS, HEADDIM)
            dt_proc = jax.nn.softplus(dt + dt_bias)
            A = -jnp.exp(A_log)
            dA = dt_proc * A
            y = ssd_chunked(x, dA, B, C, CHUNK)
            y = y + x * D[None, None, :, None]
            y = y.reshape(b, s, D_INNER)
            z_flat = z.reshape(b, s, D_INNER)
            y = y * jax.nn.silu(z_flat)
            return u + jnp.einsum('bse,de->bsd', y, out_proj_w)
        key = jax.random.key(seed)
        ks = jax.random.split(key, 6)
        u = jax.random.normal(ks[0], (BATCH, SEQ, DIM), dtype=jnp.float32)
        in_proj_w = jax.random.normal(ks[1], (D_PROJ, DIM), dtype=jnp.float32) * 0.02
        out_proj_w = jax.random.normal(ks[2], (DIM, D_INNER), dtype=jnp.float32) * 0.02
        D = jnp.ones((NHEADS,), dtype=jnp.float32)
        dt_bias = jax.random.normal(ks[3], (NHEADS,), dtype=jnp.float32) * 0.1
        A_log = jnp.log(0.5 + jax.random.uniform(ks[4], (NHEADS,), dtype=jnp.float32) * 0.5)
        bnorm_w = jnp.ones((D_STATE,), dtype=jnp.float32)
        cnorm_w = jnp.ones((D_STATE,), dtype=jnp.float32)
        ln_w = jnp.ones((DIM,), dtype=jnp.float32)
        ln_b = jnp.zeros((DIM,), dtype=jnp.float32)
        return {'u': u, 'in_proj_w': in_proj_w, 'out_proj_w': out_proj_w, 'D': D, 'dt_bias': dt_bias, 'A_log': A_log, 'bnorm_w': bnorm_w, 'cnorm_w': cnorm_w, 'ln_w': ln_w, 'ln_b': ln_b}
    _L0_attn_in = _L0_attn_setup()

    def _L0_ffn_setup():
        import jax, jax.numpy as jnp
        import numpy as np
        B, S, EMB = (4, 256, 256)
        LAT, HID = (64, 128)
        E, K = (16, 8)
        SCALE = 2.5

        def _w(key, shape, fan_in):
            return jax.random.normal(key, shape, jnp.float32) * fan_in ** (-0.5)

        def _sqrelu(x):
            return jnp.square(jax.nn.relu(x))
        key = jax.random.key(seed)
        ks = jax.random.split(key, 11)
        return {'x': jax.random.normal(ks[0], (B, S, EMB), jnp.float32), 'sw1': _w(ks[1], (HID, EMB), EMB), 'swg': _w(ks[2], (HID, EMB), EMB), 'sw2': _w(ks[3], (EMB, HID), HID), 'rw1': _w(ks[4], (E, HID, LAT), LAT), 'rwg': _w(ks[5], (E, HID, LAT), LAT), 'rw2': _w(ks[6], (E, LAT, HID), HID), 'Wg': _w(ks[7], (E, EMB), EMB), 'Wdown': _w(ks[8], (LAT, EMB), EMB), 'Wup': _w(ks[9], (EMB, LAT), LAT), 'biases': jnp.zeros((E,), jnp.float32)}
    _L0_ffn_in = _L0_ffn_setup()

    def _L1_attn_setup():
        import jax, jax.numpy as jnp
        import numpy as np
        B, T, HID = (1, 256, 256)
        H = 16
        D = HID // H
        EPS = 1e-05

        def _layer_norm(x, eps=1e-05):
            mu = jnp.mean(x, axis=-1, keepdims=True)
            var = jnp.mean((x - mu) ** 2, axis=-1, keepdims=True)
            return (x - mu) * jax.lax.rsqrt(var + eps)

        def _feature_map(x, gamma, beta):
            return _layer_norm(x * gamma + beta)
        key = jax.random.key(seed)
        ks = jax.random.split(key, 8)
        s = HID ** (-0.5)
        return {'hidden_states': jax.random.normal(ks[0], (B, T, HID), jnp.float32), 'Wq': jax.random.normal(ks[1], (HID, HID), jnp.float32) * s, 'Wk': jax.random.normal(ks[2], (HID, HID), jnp.float32) * s, 'Wv': jax.random.normal(ks[3], (HID, HID), jnp.float32) * s, 'Wo': jax.random.normal(ks[4], (HID, HID), jnp.float32) * s, 'gamma': 1.0 + 0.1 * jax.random.normal(ks[5], (D,), jnp.float32), 'beta': 0.1 * jax.random.normal(ks[6], (D,), jnp.float32)}
    _L1_attn_in = _L1_attn_setup()

    def _L1_ffn_setup():
        import jax, jax.numpy as jnp
        import numpy as np
        TOP_P = 0.9
        S, B, H, I, E = (256, 4, 256, 512, 8)

        def _top_p_weights(probs, top_p):
            order = jnp.argsort(-probs, axis=-1)
            sp = jnp.take_along_axis(probs, order, axis=-1)
            cum = jnp.cumsum(sp, axis=-1)
            exceed = cum > top_p
            first_idx = jnp.argmax(exceed, axis=-1)
            first = jnp.arange(probs.shape[-1])[None, :] == first_idx[:, None]
            keep = ~exceed | first
            kept = jnp.where(keep, sp, 0.0)
            t_idx = jnp.arange(probs.shape[0])[:, None]
            return jnp.zeros_like(probs).at[t_idx, order].set(kept)
        key = jax.random.key(seed)
        ks = jax.random.split(key, 5)
        scale = 0.02
        return {'hidden_states': jax.random.normal(ks[0], (S, B, H), dtype=jnp.float32), 'router_w': jax.random.normal(ks[1], (E, H), dtype=jnp.float32) * scale, 'gate_w': jax.random.normal(ks[2], (E, I, H), dtype=jnp.float32) * scale, 'up_w': jax.random.normal(ks[3], (E, I, H), dtype=jnp.float32) * scale, 'down_w': jax.random.normal(ks[4], (E, H, I), dtype=jnp.float32) * scale}
    _L1_ffn_in = _L1_ffn_setup()
    _d = {'L0_attn_u': _L0_attn_in['u'], 'L0_attn_in_proj_w': _L0_attn_in['in_proj_w'], 'L0_attn_out_proj_w': _L0_attn_in['out_proj_w'], 'L0_attn_D': _L0_attn_in['D'], 'L0_attn_dt_bias': _L0_attn_in['dt_bias'], 'L0_attn_A_log': _L0_attn_in['A_log'], 'L0_attn_bnorm_w': _L0_attn_in['bnorm_w'], 'L0_attn_cnorm_w': _L0_attn_in['cnorm_w'], 'L0_attn_ln_w': _L0_attn_in['ln_w'], 'L0_attn_ln_b': _L0_attn_in['ln_b'], 'L0_ffn_sw1': _L0_ffn_in['sw1'], 'L0_ffn_swg': _L0_ffn_in['swg'], 'L0_ffn_sw2': _L0_ffn_in['sw2'], 'L0_ffn_rw1': _L0_ffn_in['rw1'], 'L0_ffn_rwg': _L0_ffn_in['rwg'], 'L0_ffn_rw2': _L0_ffn_in['rw2'], 'L0_ffn_Wg': _L0_ffn_in['Wg'], 'L0_ffn_Wdown': _L0_ffn_in['Wdown'], 'L0_ffn_Wup': _L0_ffn_in['Wup'], 'L0_ffn_biases': _L0_ffn_in['biases'], 'L1_attn_Wq': _L1_attn_in['Wq'], 'L1_attn_Wk': _L1_attn_in['Wk'], 'L1_attn_Wv': _L1_attn_in['Wv'], 'L1_attn_Wo': _L1_attn_in['Wo'], 'L1_attn_gamma': _L1_attn_in['gamma'], 'L1_attn_beta': _L1_attn_in['beta'], 'L1_ffn_router_w': _L1_ffn_in['router_w'], 'L1_ffn_gate_w': _L1_ffn_in['gate_w'], 'L1_ffn_up_w': _L1_ffn_in['up_w'], 'L1_ffn_down_w': _L1_ffn_in['down_w']}
    _x0 = _d['L0_attn_u']
    _d['L0_attn_u'] = jax.random.normal(jax.random.fold_in(jax.random.key(seed), 1), (4, 512, 256), dtype=_x0.dtype)
    del _x0
    return _d

def reference(L0_attn_u, L0_attn_in_proj_w, L0_attn_out_proj_w, L0_attn_D, L0_attn_dt_bias, L0_attn_A_log, L0_attn_bnorm_w, L0_attn_cnorm_w, L0_attn_ln_w, L0_attn_ln_b, L0_ffn_sw1, L0_ffn_swg, L0_ffn_sw2, L0_ffn_rw1, L0_ffn_rwg, L0_ffn_rw2, L0_ffn_Wg, L0_ffn_Wdown, L0_ffn_Wup, L0_ffn_biases, L1_attn_Wq, L1_attn_Wk, L1_attn_Wv, L1_attn_Wo, L1_attn_gamma, L1_attn_beta, L1_ffn_router_w, L1_ffn_gate_w, L1_ffn_up_w, L1_ffn_down_w):

    def _L0_attn_ref(u, in_proj_w, out_proj_w, D, dt_bias, A_log, bnorm_w, cnorm_w, ln_w, ln_b):
        import jax, jax.numpy as jnp
        import numpy as np
        DIM = 256
        D_STATE = 128
        EXPAND = 2
        HEADDIM = 64
        CHUNK = 64
        NGROUPS = 1
        D_INNER = EXPAND * DIM
        NHEADS = D_INNER // HEADDIM
        D_PROJ = D_INNER * 2 + NGROUPS * D_STATE * 2 + NHEADS
        BATCH, SEQ = (2, 512)
        EPS = 1e-05

        def segsum(x):
            T = x.shape[-1]
            xx = jnp.broadcast_to(x[..., :, None], x.shape + (T,))
            keep = jnp.tril(jnp.ones((T, T), dtype=bool), -1)
            xx = jnp.where(keep, xx, 0.0)
            s = jnp.cumsum(xx, axis=-2)
            tri = jnp.tril(jnp.ones((T, T), dtype=bool), 0)
            return jnp.where(tri, s, -jnp.inf)

        def rms_norm(x, w):
            return x * jax.lax.rsqrt(jnp.mean(x * x, axis=-1, keepdims=True) + EPS) * w

        def layer_norm(x, w, b):
            mu = jnp.mean(x, axis=-1, keepdims=True)
            var = jnp.mean((x - mu) ** 2, axis=-1, keepdims=True)
            return (x - mu) * jax.lax.rsqrt(var + EPS) * w + b

        def ssd_chunked(x, A, B, C, chunk):
            b, s, h, p = x.shape
            n = B.shape[-1]
            if B.shape[2] < h:
                r = h // B.shape[2]
                B = jnp.repeat(B, r, axis=2)
                C = jnp.repeat(C, r, axis=2)
            c = s // chunk
            x = x.reshape(b, c, chunk, h, p)
            A = A.reshape(b, c, chunk, h).transpose(0, 3, 1, 2)
            B = B.reshape(b, c, chunk, h, n)
            C = C.reshape(b, c, chunk, h, n)
            L = jnp.exp(segsum(A))
            Y_diag = jnp.einsum('bclhn,bcshn,bhcls,bcshp->bclhp', C, B, L, x)
            A_cumsum = jnp.cumsum(A, axis=-1)
            decay_states = jnp.exp(A_cumsum[..., -1:] - A_cumsum)
            states = jnp.einsum('bclhn,bhcl,bclhp->bchpn', B, decay_states, x)
            A_chunk = jnp.pad(A_cumsum[..., -1], ((0, 0), (0, 0), (1, 0)))
            decay_chunk = jnp.exp(segsum(A_chunk))
            new_states = jnp.einsum('bhzc,bchpn->bzhpn', decay_chunk[:, :, :c, 1:c + 1], states)
            Y_off = jnp.einsum('bclhn,bchpn,bhcl->bclhp', C, new_states, jnp.exp(A_cumsum))
            return (Y_diag + Y_off).reshape(b, s, h, p)

        def mamba3_forward(u, in_proj_w, out_proj_w, D, dt_bias, A_log, bnorm_w, cnorm_w, ln_w, ln_b):
            b, s, _ = u.shape
            u_n = layer_norm(u, ln_w, ln_b)
            proj = jnp.einsum('bsd,ed->bse', u_n, in_proj_w)
            z = proj[..., :D_INNER]
            x = proj[..., D_INNER:2 * D_INNER]
            B = proj[..., 2 * D_INNER:2 * D_INNER + NGROUPS * D_STATE].reshape(b, s, NGROUPS, D_STATE)
            C = proj[..., 2 * D_INNER + NGROUPS * D_STATE:2 * D_INNER + 2 * NGROUPS * D_STATE].reshape(b, s, NGROUPS, D_STATE)
            dt = proj[..., -NHEADS:]
            B = rms_norm(B, bnorm_w)
            C = rms_norm(C, cnorm_w)
            x = x.reshape(b, s, NHEADS, HEADDIM)
            z = z.reshape(b, s, NHEADS, HEADDIM)
            dt_proc = jax.nn.softplus(dt + dt_bias)
            A = -jnp.exp(A_log)
            dA = dt_proc * A
            y = ssd_chunked(x, dA, B, C, CHUNK)
            y = y + x * D[None, None, :, None]
            y = y.reshape(b, s, D_INNER)
            z_flat = z.reshape(b, s, D_INNER)
            y = y * jax.nn.silu(z_flat)
            return u + jnp.einsum('bse,de->bsd', y, out_proj_w)
        return mamba3_forward(u, in_proj_w, out_proj_w, D, dt_bias, A_log, bnorm_w, cnorm_w, ln_w, ln_b)

    def _L0_ffn_ref(x, sw1, swg, sw2, rw1, rwg, rw2, Wg, Wdown, Wup, biases):
        import jax, jax.numpy as jnp
        import numpy as np
        B, S, EMB = (4, 256, 256)
        LAT, HID = (64, 128)
        E, K = (16, 8)
        SCALE = 2.5

        def _w(key, shape, fan_in):
            return jax.random.normal(key, shape, jnp.float32) * fan_in ** (-0.5)

        def _sqrelu(x):
            return jnp.square(jax.nn.relu(x))
        b, s, d = x.shape
        x2 = x.reshape(-1, d)
        shared = x2 @ sw1.T * _sqrelu(x2 @ swg.T) @ sw2.T
        xl = x2 @ Wdown.T
        probas = jax.nn.sigmoid(x2 @ Wg.T)
        _, idx = jax.lax.top_k(probas + biases, K)
        p = jnp.take_along_axis(probas, idx, axis=-1)
        p = p / p.sum(-1, keepdims=True) * SCALE
        T = x2.shape[0]
        w_dense = jnp.zeros((T, E), x2.dtype).at[jnp.arange(T)[:, None], idx].add(p)
        acc = jnp.zeros_like(xl)
        for e in range(E):
            ye = xl @ rw1[e].T * _sqrelu(xl @ rwg[e].T) @ rw2[e].T
            acc = acc + w_dense[:, e:e + 1] * ye
        out = shared + acc @ Wup.T
        return out.reshape(b, s, d)

    def _L1_attn_ref(hidden_states, Wq, Wk, Wv, Wo, gamma, beta):
        import jax, jax.numpy as jnp
        import numpy as np
        B, T, HID = (1, 256, 256)
        H = 16
        D = HID // H
        EPS = 1e-05

        def _layer_norm(x, eps=1e-05):
            mu = jnp.mean(x, axis=-1, keepdims=True)
            var = jnp.mean((x - mu) ** 2, axis=-1, keepdims=True)
            return (x - mu) * jax.lax.rsqrt(var + eps)

        def _feature_map(x, gamma, beta):
            return _layer_norm(x * gamma + beta)
        b, t, _ = hidden_states.shape
        q = (hidden_states @ Wq.T).reshape(b, t, H, D)
        k = (hidden_states @ Wk.T).reshape(b, t, H, D)
        v = (hidden_states @ Wv.T).reshape(b, t, H, D)
        q = _feature_map(q, gamma, beta)
        k = _feature_map(k, gamma, beta)
        q = q * D ** (-0.5)
        attn = jnp.einsum('bqhd,bkhd->bhqk', q, k) ** 2
        mask = jnp.tril(jnp.ones((t, t), dtype=bool))
        attn = jnp.where(mask, attn, 0.0)
        o = jnp.einsum('bhqk,bkhd->bqhd', attn, v)
        z = jnp.sum(attn, axis=-1)
        o = o / (jnp.swapaxes(z, 1, 2)[..., None] + EPS)
        o = o.reshape(b, t, H * D)
        return o @ Wo.T

    def _L1_ffn_ref(hidden_states, router_w, gate_w, up_w, down_w):
        import jax, jax.numpy as jnp
        import numpy as np
        TOP_P = 0.9
        S, B, H, I, E = (256, 4, 256, 512, 8)

        def _top_p_weights(probs, top_p):
            order = jnp.argsort(-probs, axis=-1)
            sp = jnp.take_along_axis(probs, order, axis=-1)
            cum = jnp.cumsum(sp, axis=-1)
            exceed = cum > top_p
            first_idx = jnp.argmax(exceed, axis=-1)
            first = jnp.arange(probs.shape[-1])[None, :] == first_idx[:, None]
            keep = ~exceed | first
            kept = jnp.where(keep, sp, 0.0)
            t_idx = jnp.arange(probs.shape[0])[:, None]
            return jnp.zeros_like(probs).at[t_idx, order].set(kept)
        s, b, h = hidden_states.shape
        x = hidden_states.reshape(-1, h)
        probs = jax.nn.softmax(x @ router_w.T, axis=-1)
        w = _top_p_weights(probs, TOP_P)
        out = jnp.zeros_like(x)
        n_exp = router_w.shape[0]
        for e in range(n_exp):
            g = jax.nn.silu(x @ gate_w[e].T)
            u = x @ up_w[e].T
            y = g * u @ down_w[e].T
            out = out + y * w[:, e:e + 1]
        return out.reshape(s, b, h)
    x = L0_attn_u
    x = x + _layernorm(_L0_attn_ref(_layernorm(x, axis=-1), L0_attn_in_proj_w, L0_attn_out_proj_w, L0_attn_D, L0_attn_dt_bias, L0_attn_A_log, L0_attn_bnorm_w, L0_attn_cnorm_w, L0_attn_ln_w, L0_attn_ln_b), axis=-1)
    x = x + _layernorm(_L0_ffn_ref(_layernorm(x, axis=-1), L0_ffn_sw1, L0_ffn_swg, L0_ffn_sw2, L0_ffn_rw1, L0_ffn_rwg, L0_ffn_rw2, L0_ffn_Wg, L0_ffn_Wdown, L0_ffn_Wup, L0_ffn_biases), axis=-1)
    x = x + _layernorm(_L1_attn_ref(_layernorm(x, axis=-1), L1_attn_Wq, L1_attn_Wk, L1_attn_Wv, L1_attn_Wo, L1_attn_gamma, L1_attn_beta), axis=-1)
    x = x + _layernorm(_L1_ffn_ref(_layernorm(x, axis=-1), L1_ffn_router_w, L1_ffn_gate_w, L1_ffn_up_w, L1_ffn_down_w), axis=-1)
    return x

_drawn_inputs = setup_inputs


def setup_inputs(seed=0):
    import zlib

    import numpy as np

    out = dict(_drawn_inputs(seed))
    spreads = {'L0_attn_D': (1.0, 0.2),
     'L0_attn_bnorm_w': (1.0, 0.2),
     'L0_attn_cnorm_w': (1.0, 0.2),
     'L0_attn_ln_w': (1.0, 0.2),
     'L0_attn_ln_b': (0.0, 0.1),
     'L0_ffn_biases': (0.0, 0.1)}
    factors = {}
    for name, (base, spread) in spreads.items():
        noise = np.random.default_rng([zlib.crc32(name.encode()), seed]).standard_normal(out[name].shape)
        drawn = base * np.exp(spread * noise) if base else spread * noise
        out[name] = jnp.asarray(drawn.astype(out[name].dtype))
    for name, factor in factors.items():
        out[name] = (out[name] * factor).astype(out[name].dtype)
    return out
```

```python
from contextlib import ExitStack
from functools import partial

import concourse.bass as bass
from concourse import mybir

F32 = mybir.dt.float32
F32R = mybir.dt.float32r
ALU = mybir.AluOpType
ACT = mybir.ActivationFunctionType
AX = mybir.AxisListType

P = 128
HID = 256
KH = HID // P
TOK = 2048
NT = TOK // P
NB = 4
TB = NT // NB
GT = TB * P
EPS = 1e-5


class Core:

    def __init__(self, nc, ctx, keep, tag):
        self.nc, self.ctx, self.keep, self.tag = nc, ctx, keep, tag

    def sb(self, name, shape, dt=F32):
        return self.ctx.enter_context(self.nc.sbuf_tensor(f"{self.tag}_{name}", shape, dt))

    def ps(self, name, shape, dt=F32):
        return self.ctx.enter_context(self.nc.psum_tensor(f"{self.tag}_{name}", shape, dt))

    def sem(self, name):
        self.keep.append(self.nc.alloc_semaphore(f"{self.tag}_{name}"))
        return self.keep[-1]


class Tally:

    def __init__(self, eng):
        self.eng, self.n = eng, {}

    def __call__(self, ins, sem, by=1):
        ins.then_inc(sem, by)
        self.n[sem.name] = self.n.get(sem.name, 0) + by
        return ins

    def settle(self, sem):
        self.eng.wait_ge(sem, self.n[sem.name])


def three_pass(pe, out, w_hi, w_lo, x_hi, x_lo, start, stop):
    pe.matmul(out, w_hi, x_hi, start=start, stop=False, skip_group_check=True)
    pe.matmul(out, w_hi, x_lo, start=False, stop=False, skip_group_check=True)
    return pe.matmul(out, w_lo, x_hi, start=False, stop=stop, skip_group_check=True)


def inverse_root(pool, v, half, sem_eps, count, sem_done, eps=EPS):
    pool.tensor_scalar(v, v, eps, None, ALU.add).then_inc(sem_eps, 1)
    pool.wait_ge(sem_eps, count)
    pool.tensor_tensor(v, v, half, ALU.pow).then_inc(sem_done, 1)


class FirstGroup:

    def __init__(self, c, x, half):
        self.x, self.half = x, half
        self.stats = c.sb("first_stats", [P, TB, 6])
        self.moments = c.sb("first_moments", [P, TB, 2])
        self.s_stats = c.sem("first_stats_done")
        self.s_moments = c.sem("first_moments_done")
        self.s_eps = c.sem("first_eps_added")
        self.s_rstd = c.sem("first_rstd_ready")

    def take_stats(self, dve):
        for t in range(TB):
            dve.bn_stats(self.stats[:, t, :], self.x[:, t, :]).then_inc(self.s_stats, 1)
        dve.wait_ge(self.s_stats, TB)
        for t in range(TB):
            dve.bn_aggr(self.moments[:, t, :], self.stats[:, t, :]).then_inc(self.s_moments, 1)

    def root(self, pool):
        pool.wait_ge(self.s_moments, TB)
        inverse_root(pool, self.moments[:, :, 1], self.half[:, 0:TB], self.s_eps, 1, self.s_rstd)


class Prep:

    def __init__(self, c, x, xT_hi, xT_lo, ident, half, first, banks, claim=None):
        self.half, self.first = half, first
        self.x, self.xT_hi, self.xT_lo, self.ident = x, xT_hi, xT_lo, ident
        self.bank = banks if callable(banks) else lambda b, k: banks[k % len(banks)]
        self.claim = claim or (lambda pe, b, k: self.wait_read(pe, KH * b + k - len(banks)))
        self.xn = c.sb("xn", [P, 2, TB, HID])
        self.stats = c.sb("prep_stats", [P, NT, 6])
        self.moments = c.sb("prep_moments", [P, NT, 2])
        self.s_stats = c.sem("prep_stats_done")
        self.s_moments = c.sem("prep_moments_done")
        self.s_eps = c.sem("prep_eps_added")
        self.s_rstd = c.sem("prep_rstd_ready")
        self.s_xn = c.sem("xn_ready")
        self.s_turned = c.sem("xT_turned")
        self.s_hi = c.sem("xT_hi_ready")
        self.s_lo = c.sem("xT_lo_ready")

    def take_stats(self, dve, tally, b):
        for t in range(TB):
            ins = dve.bn_stats(self.stats[:, b * TB + t, :], self.x[:, b * TB + t, :])
        tally(ins, self.s_stats)
        tally.settle(self.s_stats)
        for t in range(TB):
            ins = dve.bn_aggr(self.moments[:, b * TB + t, :], self.stats[:, b * TB + t, :])
        tally(ins, self.s_moments)

    def take_xn(self, dve, tally, b):
        if b:
            dve.wait_ge(self.s_rstd, b)
            moments = self.moments[:, b * TB:(b + 1) * TB, :]
        else:
            dve.wait_ge(self.first.s_rstd, 1)
            moments = self.first.moments
        if b >= 2:
            dve.wait_ge(self.s_turned, KH * (b - 1))
        for t in range(TB):
            ins = dve.tensor_scalar(self.xn[:, b % 2, t, :], self.x[:, b * TB + t, :],
                                    moments[:, t, 0:1], moments[:, t, 1:2],
                                    ALU.subtract, ALU.mult)
        tally(ins, self.s_xn)
        tally.settle(self.s_xn)

    def root(self, pool, b):
        pool.wait_ge(self.s_moments, b)
        inverse_root(pool, self.moments[:, b * TB:(b + 1) * TB, 1], self.half[:, 0:TB], self.s_eps, b, self.s_rstd)

    def wait_read(self, pe, i):
        if i >= 0:
            pe.wait_ge(self.s_lo, i + 1)

    def turn(self, pe, b, blocks=range(KH)):
        pe.wait_ge(self.s_xn, b + 1)
        for k in blocks:
            self.claim(pe, b, k)
            for t in range(TB):
                ins = pe.transpose(self.bank(b, k)[:, t * P:(t + 1) * P],
                                   self.xn[:, b % 2, t, k * P:(k + 1) * P], self.ident[:, :])
            ins.then_inc(self.s_turned, 1)

    def take_hi(self, act, b, blocks=range(KH)):
        for k in blocks:
            act.wait_ge(self.s_turned, KH * b + k + 1)
            act.activation(self.xT_hi[:, k, b * GT:(b + 1) * GT], self.bank(b, k)[:, :], ACT.Copy)\
               .then_inc(self.s_hi, 1)

    def take_lo(self, dve, tally, b, blocks=range(KH)):
        for k in blocks:
            dve.wait_ge(self.s_hi, KH * b + k + 1)
            tally(dve.tensor_tensor(self.xT_lo[:, k, b * GT:(b + 1) * GT], self.bank(b, k)[:, :],
                                    self.xT_hi[:, k, b * GT:(b + 1) * GT], ALU.subtract), self.s_lo)


class AddNorm:

    def __init__(self, c, x, half):
        self.x, self.half = x, half
        self.stats = c.sb("out_stats", [P, TB, 6])
        self.moments = c.sb("out_moments", [P, TB, 2])
        self.normed = c.sb("out_normed", [P, TB, HID])
        self.s_stats = c.sem("out_stats_done")
        self.s_moments = c.sem("out_moments_done")
        self.s_eps = c.sem("out_eps_added")
        self.s_rstd = c.sem("out_rstd_ready")
        self.s_normed = c.sem("out_normed_done")
        self.s_x = c.sem("x_updated")

    def add(self, dve, tally, b, v):
        self.take_stats(dve, tally, v)
        self.add_normed(dve, tally, b, v)

    def take_stats(self, dve, tally, v):
        for t in range(TB):
            ins = dve.bn_stats(self.stats[:, t, :], v[t])
        tally(ins, self.s_stats)
        tally.settle(self.s_stats)
        for t in range(TB):
            ins = dve.bn_aggr(self.moments[:, t, :], self.stats[:, t, :])
        tally(ins, self.s_moments)

    def add_normed(self, dve, tally, b, v):
        self.norm_only(dve, tally, b, v)
        tally.settle(self.s_normed)
        self.update_x(dve, b)
        tally.n[self.s_x.name] = b + 1
        tally.settle(self.s_x)

    def norm_only(self, dve, tally, b, v):
        dve.wait_ge(self.s_rstd, b + 1)
        if b:
            dve.wait_ge(self.s_x, b)
        for t in range(TB):
            ins = dve.tensor_scalar(self.normed[:, t, :], v[t], self.moments[:, t, 0:1],
                                    self.moments[:, t, 1:2], ALU.subtract, ALU.mult)
        tally(ins, self.s_normed)

    def update_x(self, engine, b):
        engine.wait_ge(self.s_normed, b + 1)
        xg = self.x[:, b * TB:(b + 1) * TB, :]
        engine.tensor_tensor(xg, xg, self.normed[:, :, :], ALU.add).then_inc(self.s_x, 1)

    def root(self, pool, b):
        pool.wait_ge(self.s_moments, b + 1)
        inverse_root(pool, self.moments[:, :, 1], self.half[:, 0:TB], self.s_eps, b + 1, self.s_rstd)


E4 = 8
I4 = 512
M4 = I4 // P
W4 = 2 * KH * I4 + M4 * HID
TOP_P = 0.9


def top_p_ffn(nc, keep, x, xT_hi, xT_lo, ident, half, first, w_dram, router_dram, out_dram):
    with ExitStack() as ctx:
        c = Core(nc, ctx, keep, "ffn1")
        bank = [c.ps(f"bank{i}", [P, 512]) for i in range(8)]
        turned = (bank[0], bank[1], bank[4], bank[5])
        prep = Prep(c, x, xT_hi, xT_lo, ident, half, first, lambda b, k: turned[(KH * b + k) % 4],
                    lambda pe, b, k: prep.wait_read(pe, KH * b + k - 4))
        addn = AddNorm(c, x, half)
        rw = c.sb("rw", [P, KH, E4])
        rw_hi, rw_lo = c.sb("rw_hi", [P, KH, E4], F32R), c.sb("rw_lo", [P, KH, E4], F32R)
        lgT = c.sb("lgT", [E4, 2, GT])
        p = c.sb("p", [P, NT, E4])
        row = c.sb("row", [P, NT, 1])
        pair = c.sb("pair", [P, NT, E4, E4])
        w = c.sb("w", [P, NT, E4])
        staged = c.sb("staged", [P, W4])
        w_hi, w_lo = c.sb("w_hi", [P, 2, W4], F32R), c.sb("w_lo", [P, 2, W4], F32R)
        sg = c.sb("sg", [P, 2, GT])
        h = c.sb("h", [P, 2, GT])
        h_hi, h_lo = c.sb("h_hi", [P, 2, M4, GT], F32R), c.sb("h_lo", [P, 2, M4, GT], F32R)
        acc = c.sb("acc", [P, NT, HID])
        g_bank, u_bank = bank[0:2], bank[2:4]
        y_bank = [bank[4:6], bank[6:8]]

        s_rw = c.sem("router_w_landed")
        s_rws = c.sem("router_w_split")
        s_const = c.sem("constants_set")
        s_lg = c.sem("logits_full")
        s_lgc = c.sem("logits_copied")
        s_lgT = c.sem("logits_turned")
        s_p = c.sem("logits_ready")
        s_ms = c.sem("max_subtracted")
        s_exp = c.sem("exp_done")
        s_step = c.sem("router_step")
        s_w = c.sem("weights_of_tokens")
        s_seen = c.sem("weights_seen")
        s_land = c.sem("expert_landed")
        s_hi = c.sem("expert_hi_half")
        s_split = c.sem("expert_split")
        s_g = c.sem("gate_full")
        s_u = c.sem("up_full")
        s_silu = c.sem("silu_done")
        s_h = c.sem("h_done")
        s_hh = c.sem("h_hi_done")
        s_hl = c.sem("h_lo_done")
        s_y = c.sem("y_full")
        s_acc = c.sem("acc_done")
        s_out = c.sem("out_written")

        def gate_w(half, e2, k, m):
            return half[:, e2, k * I4 + m * P:k * I4 + (m + 1) * P]

        def up_w(half, e2, k, m):
            return half[:, e2, (KH + k) * I4 + m * P:(KH + k) * I4 + (m + 1) * P]

        def down_w(half, e2, m):
            return half[:, e2, 2 * KH * I4 + m * HID:2 * KH * I4 + (m + 1) * HID]

        ORDER = [("up", 0), ("up", 1), ("down", 0), ("up", 2), ("down", 1), ("up", 3), ("down", 2), ("down", 3)]
        AFTER = {3: ("stats", 0), 4: ("add", 0), 5: ("stats", 1), 6: ("add", 1), 7: ("stats", 2)}
        FREE = 2
        ACC_FREE = 4
        Y_FREE = 2 * TB

        with nc.Block() as block:
            @block.sync
            def _(sp):
                sp.dma_start(rw[:, :, :], router_dram).then_inc(s_rw, 16)
                sp.dma_start(staged[:, :], w_dram[0]).then_inc(s_land, 16)
                with sp.Fori(1, E4) as e:
                    sp.wait_ge(s_split, e)
                    sp.dma_start(staged[:, :], w_dram[bass.ds(e, 1)].rearrange("a p n -> p (a n)")).then_inc(s_land, 16)
                for b in range(NB):
                    sp.wait_ge(addn.s_x, b + 1)
                    sp.dma_start(out_dram[:, b * TB:(b + 1) * TB, :], x[:, b * TB:(b + 1) * TB, :])\
                      .then_inc(s_out, 16)
                sp.wait_ge(s_out, 16 * NB)

            @block.gpsimd
            def _(pool):
                def split(e, e2, halved=False):
                    if not halved:
                        pool.wait_ge(s_land, 16 * (e + 1))
                        pool.sem_inc(s_seen, 1)
                        for q in range(0, W4, 512):
                            ins = pool.tensor_scalar(w_hi[:, e2, q:q + 512], staged[:, q:q + 512], 1.0, None, ALU.mult)
                        ins.then_inc(s_hi, 1)
                    pool.wait_ge(s_hi, e + 1)
                    for q in range(0, W4, 512):
                        ins = pool.tensor_tensor(w_lo[:, e2, q:q + 512], staged[:, q:q + 512],
                                                 w_hi[:, e2, q:q + 512], ALU.subtract)
                    ins.then_inc(s_split, 1)

                for b in range(1, NB):
                    prep.root(pool, b)
                split(0, 0, halved=True)
                pool.memset(acc[:, :, :], 0.0).then_inc(s_const, 1)
                split(1, 1)
                with pool.Fori(0, E4 // 2 - 1) as ep:
                    for e2 in range(2):
                        pool.wait_ge(s_y, (ep * 2 + e2 + 1) * NT + Y_FREE)
                        split(ep * 2 + (e2 + 2), e2)
                for b in range(NB):
                    addn.root(pool, b)

            @block.scalar
            def _(act):
                act.sem_inc(s_silu, FREE)
                act.sem_inc(s_hh, FREE)
                act.wait_ge(s_rw, 16)
                act.activation(rw_hi[:, :, :], rw[:, :, :], ACT.Copy).then_inc(s_rws, 1)
                for b in range(NB + 1):
                    if b < NB:
                        prep.take_hi(act, b)
                    if b == 0:
                        act.wait_ge(s_land, 16)
                        for q in range(0, W4, 512):
                            ins = act.activation(w_hi[:, 0, q:q + 512], staged[:, q:q + 512], ACT.Copy)
                        ins.then_inc(s_hi, 1)
                        continue
                    b -= 1
                    act.wait_ge(s_lg, b + 1)
                    if b >= 2:
                        act.wait_ge(s_lgT, b - 1)
                    act.activation(lgT[:, b % 2, :], bank[2][0:E4, :], ACT.Copy).then_inc(s_lgc, 1)
                act.wait_ge(s_ms, 1)
                act.activation(p[:, :, :], p[:, :, :], ACT.Exp).then_inc(s_exp, 1)

                with act.Fori(0, E4 // 2) as ep:
                    for e2 in range(2):
                        for tb in range(NB):
                            for m in range(M4):
                                n = ep * (2 * NB * M4) + (e2 * NB + tb) * M4 + m
                                act.wait_ge(s_g, n + 1)
                                act.wait_ge(s_h, n + 1)
                                act.activation(sg[:, m % 2, :], g_bank[m % 2][:, :], ACT.Silu).then_inc(s_silu, 1)
                                act.wait_ge(s_h, n + 1 + FREE)
                                if m == 0:
                                    act.wait_ge(s_y, (ep * 2 * NB + e2 * NB + tb) * TB + TB)
                                act.activation(h_hi[:, tb % 2, m, :], h[:, m % 2, :], ACT.Copy).then_inc(s_hh, 1)

            @block.vector
            def _(dve):
                tally = Tally(dve)
                dve.sem_inc(s_h, FREE)
                dve.sem_inc(s_acc, ACC_FREE)
                prep.take_xn(dve, tally, 0)
                prep.take_stats(dve, tally, 1)
                dve.wait_ge(s_rws, 1)
                dve.tensor_tensor(rw_lo[:, :, :], rw[:, :, :], rw_hi[:, :, :], ALU.subtract).then_inc(s_rws, 1)
                prep.take_lo(dve, tally, 0)
                prep.take_xn(dve, tally, 1)
                for b in range(2, NB):
                    prep.take_stats(dve, tally, b)
                for b in range(NB + 2):
                    if 0 < b < NB:
                        prep.take_lo(dve, tally, b)
                    if b + 2 < NB:
                        prep.take_xn(dve, tally, b + 2)
                    if b < 2:
                        continue
                    b -= 2
                    dve.wait_ge(s_lgT, b + 1)
                    tally(dve.tensor_copy(p[:, b * TB:(b + 1) * TB, :],
                                          bank[3][:, 0:TB * E4].rearrange("p (t e) -> p t e", e=E4)), s_p)
                tally.settle(s_p)

                def step(ins):
                    tally(ins, s_step)
                    tally.settle(s_step)

                step(dve.tensor_reduce(row[:, :, 0], p[:, :, :], AX.X, ALU.max))
                dve.tensor_tensor(p[:, :, :], p[:, :, :], row[:, :, :].broadcast_to([P, NT, E4]), ALU.subtract)\
                   .then_inc(s_ms, 1)
                dve.wait_ge(s_exp, 1)
                pj = p[:, :, :].unsqueeze(2).broadcast_to([P, NT, E4, E4])
                pe_ = p[:, :, :].unsqueeze(3).broadcast_to([P, NT, E4, E4])

                def route(part):
                    if part == 0:
                        dve.wait_ge(s_exp, 1)
                        step(dve.tensor_reduce(row[:, :, 0], p[:, :, :], AX.X, ALU.add))
                        step(dve.reciprocal(row[:, :, 0], row[:, :, 0]))
                    if part == 1:
                        step(dve.tensor_tensor(p[:, :, :], p[:, :, :], row[:, :, :].broadcast_to([P, NT, E4]), ALU.mult))
                    if part == 2:
                        step(dve.tensor_tensor(pair[:, :, :, :], pj, pe_, ALU.is_gt))
                    if part == 3:
                        for e in range(1, E4):
                            ins = dve.tensor_tensor(pair[:, :, e, 0:e], p[:, :, 0:e],
                                                    p[:, :, e:e + 1].broadcast_to([P, NT, e]), ALU.is_ge)
                        step(ins)
                    if part == 4:
                        step(dve.tensor_tensor(pair[:, :, :, :], pair[:, :, :, :], pj, ALU.mult))
                    if part == 5:
                        step(dve.tensor_reduce(w[:, :, :], pair[:, :, :, :], AX.X, ALU.add))
                    if part == 6:
                        step(dve.scalar_tensor_tensor(w[:, :, :], w[:, :, :], TOP_P, p[:, :, :], ALU.is_le, ALU.mult))

                def pair_of_experts(ep, first=False, last=False):
                    for e2 in range(2):
                        for at, (what, tb) in enumerate(ORDER):
                            if last and e2 == 1 and at in AFTER:
                                todo, b = AFTER[at]
                                out = [acc[:, b * TB + t, :] for t in range(TB)]
                                if todo == "stats":
                                    dve.wait_ge(s_acc, (E4 - 1) * NB + b + 1 + ACC_FREE)
                                    addn.take_stats(dve, tally, out)
                                else:
                                    addn.add_normed(dve, tally, b, out)
                            done = ep * (2 * NB) + (e2 * NB + tb)
                            if what == "up":
                                for m in range(M4):
                                    n = done * M4 + m
                                    dve.wait_ge(s_u, n + 1)
                                    dve.wait_ge(s_silu, n + 1 + FREE)
                                    dve.wait_ge(s_hh, n + 1)
                                    dve.tensor_tensor(h[:, m % 2, :], sg[:, m % 2, :], u_bank[m % 2][:, :],
                                                      ALU.mult).then_inc(s_h, 1)
                                    dve.wait_ge(s_hh, n + 1 + FREE)
                                    dve.tensor_tensor(h_lo[:, tb % 2, m, :], h[:, m % 2, :], h_hi[:, tb % 2, m, :],
                                                      ALU.subtract).then_inc(s_hl, 1)
                                    if first and e2 == 0:
                                        route(tb * M4 + m)
                            else:
                                if first and e2 == 0 and tb == 0:
                                    dve.wait_ge(s_const, 1)
                                dve.wait_ge(s_acc, done + 1)
                                for t in range(TB):
                                    if t % 2 == 0:
                                        dve.wait_ge(s_y, done * TB + t + 2 + Y_FREE)
                                    a = acc[:, tb * TB + t, :]
                                    ins = dve.scalar_tensor_tensor(
                                        a, y_bank[tb % 2][t // 2][:, (t % 2) * HID:(t % 2 + 1) * HID],
                                        w[:, tb * TB + t, bass.ds(ep * 2 + e2, 1)], a, ALU.mult, ALU.add)
                                ins.then_inc(s_acc, 1)

                pair_of_experts(0, first=True)
                with dve.Fori(1, E4 // 2 - 1) as ep:
                    pair_of_experts(ep)
                pair_of_experts(E4 // 2 - 1, last=True)
                addn.add_normed(dve, tally, NB - 2, [acc[:, (NB - 2) * TB + t, :] for t in range(TB)])
                dve.wait_ge(s_acc, E4 * NB + ACC_FREE)
                addn.add(dve, tally, NB - 1, [acc[:, (NB - 1) * TB + t, :] for t in range(TB)])

            @block.tensor
            def _(pe):
                pe.sem_inc(s_y, Y_FREE)
                for n in range(NB + 2):
                    if n < NB:
                        prep.turn(pe, n)
                    b = n - 1
                    if 0 <= b < NB:
                        if b == 0:
                            pe.wait_ge(s_rws, 2)
                        pe.wait_ge(prep.s_lo, KH * (b + 1))
                        if b:
                            pe.wait_ge(s_lgc, b)
                        for k in range(KH):
                            blk = slice(b * GT, (b + 1) * GT)
                            ins = three_pass(pe, bank[2][0:E4, :], rw_hi[:, k, :], rw_lo[:, k, :],
                                             xT_hi[:, k, blk], xT_lo[:, k, blk], k == 0, k == KH - 1)
                        ins.then_inc(s_lg, 1)
                    b = n - 2
                    if b >= 0:
                        pe.wait_ge(s_lgc, b + 1)
                        if b:
                            pe.wait_ge(s_p, b)
                        for t in range(TB):
                            ins = pe.transpose(bank[3][:, t * E4:(t + 1) * E4], lgT[:, b % 2, t * P:(t + 1) * P],
                                               ident[0:E4, 0:E4])
                        ins.then_inc(s_lgT, 1)
                pe.wait_ge(s_p, NB)

                with pe.Fori(0, E4 // 2) as ep:
                    for e2 in range(2):
                        pe.wait_ge(s_split, ep * 2 + e2 + 1)
                        for what, tb in ORDER:
                            done = ep * (2 * NB) + (e2 * NB + tb)
                            blk = slice(tb * GT, (tb + 1) * GT)
                            if what == "up":
                                for m in range(M4):
                                    n = done * M4 + m
                                    for wt, banks, free, full in ((gate_w, g_bank, s_silu, s_g),
                                                                  (up_w, u_bank, s_h, s_u)):
                                        pe.wait_ge(free, n + 1)
                                        for k in range(KH):
                                            ins = three_pass(pe, banks[m % 2][:, :], wt(w_hi, e2, k, m),
                                                             wt(w_lo, e2, k, m), xT_hi[:, k, blk],
                                                             xT_lo[:, k, blk], k == 0, k == KH - 1)
                                        ins.then_inc(full, 1)
                            else:
                                pe.wait_ge(s_hl, done * M4 + M4)
                                pe.wait_ge(s_acc, done + ACC_FREE - 1)
                                for t in range(TB):
                                    y = y_bank[tb % 2][t // 2][:, (t % 2) * HID:(t % 2 + 1) * HID]
                                    for m in range(M4):
                                        ins = three_pass(pe, y, h_hi[:, tb % 2, m, t * P:(t + 1) * P],
                                                         h_lo[:, tb % 2, m, t * P:(t + 1) * P],
                                                         down_w(w_hi, e2, m), down_w(w_lo, e2, m),
                                                         m == 0, m == M4 - 1)
                                    ins.then_inc(s_y, 1)


E2 = 16
TOP_K = 8
LAT = 64
HID2 = 128
ITEMS2 = E2 + 1
ROUTE_SCALE = 2.5
COLS2, W2 = {}, 0
for _name, _n in (("router", KH * E2), ("shrink", KH * P), ("shared_up", KH * HID2), ("shared_gate", KH * HID2),
                  ("shared_down", HID), ("up", E2 * HID2), ("gate", E2 * HID2), ("grow", HID)):
    COLS2[_name] = W2
    W2 += _n
SPLIT2 = W2
W2 += E2 * LAT


def routed_ffn(nc, keep, x, xT_hi, xT_lo, ident, half, first, next_first, staged, staged_landed, bias_dram):
    with ExitStack() as ctx:
        c = Core(nc, ctx, keep, "ffn0")
        bank = [c.ps(f"bank{i}", [P, 512]) for i in range(8)]
        g_bank, u_bank, r_bank, acc_bank, misc = bank[0:2], bank[2:4], bank[4:6], bank[6], bank[7]
        prep = Prep(c, x, xT_hi, xT_lo, ident, half, first, lambda b, k: g_bank[0] if (b, k) == (0, 1) else misc,
                    lambda pe, b, k: b and prep.wait_read(pe, KH * b + k - 1))
        addn = AddNorm(c, x, half)
        def xl_bank(b):
            return misc if b else u_bank[0]

        N = NB * ITEMS2
        LAG = 4
        RING = 5
        BACK = {5: "V", 6: "U", 8: "W"}
        FRONT = {1: "X0", 3: "X1", 7: "F1a", 9: "F1b", 10: "F2a", 11: "F2b", 12: "F3a", 13: "F3b", 15: "F4"}

        w_hi, w_lo = c.sb("w_hi", [P, SPLIT2], F32R), c.sb("w_lo", [P, SPLIT2], F32R)
        down = c.sb("down", [P, E2, 2, LAT], F32R)
        sel = c.sb("sel", [2 * E2, E2, P], F32R)
        keep_x = c.sb("keep_x", [P, 1])
        keep_w = c.sb("keep_w", [2 * E2, 1])
        bias = c.sb("bias", [P, E2])
        probT = c.sb("probT", [E2, 2, GT])
        x_hi = c.sb("x_hi", [P, GT], F32R)
        xs = c.sb("xs", [P, 2, GT], F32R)
        prob = c.sb("prob", [P, TB, E2])
        score = c.sb("score", [P, TB, E2])
        best = c.sb("best", [P, TB, TOP_K])
        rest = c.sb("rest", [P, TB, E2])
        total = c.sb("total", [P, TB, 1])
        wt = c.sb("wt", [P, 2, TB, 2, E2])
        wT_hi = c.sb("wT_hi", [2 * E2, GT], F32R)
        ws = c.sb("ws", [2 * E2, 2, GT], F32R)
        h = c.sb("h", [P, 4, GT])
        sel32 = h[0:2 * E2, :, :].rearrange("p a (b n) -> p (a b) n", n=P)
        h_hi, h_lo = c.sb("h_hi", [P, RING, GT], F32R), c.sb("h_lo", [P, RING, GT], F32R)
        s_hi, s_lo = c.sb("s_hi", [P, 2, GT], F32R), c.sb("s_lo", [P, 2, GT], F32R)
        a_hi, a_lo = c.sb("a_hi", [P, GT], F32R), c.sb("a_lo", [P, GT], F32R)
        r, q, qu = (staged[:, i * 2 * GT:(i + 1) * 2 * GT].rearrange("p (a n) -> p a n", a=2) for i in range(3))
        v = staged[:, 6 * GT:6 * GT + 2 * TB * HID].rearrange("p (a t n) -> p a t n", a=2, t=TB)

        s_land = c.sem("bias_landed")
        s_const = c.sem("constants")
        s_selr = c.sem("selector_ready")
        s_whi = c.sem("weights_hi")
        s_wlo = c.sem("weights_lo")
        s_wlate = c.sem("later_weights_lo")
        s_lg = c.sem("logits_full")
        s_prT = c.sem("probT_ready")
        s_xl = c.sem("xl_full")
        s_xhi = c.sem("xl_hi_ready")
        s_xs = c.sem("xs_ready")
        s_pt = c.sem("probs_turned")
        s_pr = c.sem("probs_copied")
        s_step = c.sem("router_step")
        s_wt = c.sem("token_weights")
        s_wTf = c.sem("token_weights_turned")
        s_wThi = c.sem("token_weights_hi")
        s_ws = c.sem("ws_ready")
        s_g = c.sem("gate_full")
        s_u = c.sem("up_full")
        s_b = c.sem("row_weight_full")
        s_r = c.sem("relu_done")
        s_q = c.sem("square_done")
        s_qu = c.sem("squared_times_up")
        s_h = c.sem("h_done")
        s_hh = c.sem("h_hi_done")
        s_hl = c.sem("h_lo_done")
        s_d = c.sem("down_done")
        s_ahi = c.sem("acc_hi_done")
        s_alo = c.sem("acc_lo_done")
        s_v = c.sem("v_full")
        s_vc = c.sem("v_copied")

        def wcol(half_, name, i=0, n=P):
            return half_[:, COLS2[name] + i * n:COLS2[name] + (i + 1) * n]

        def steps():
            for f in FRONT.values():
                yield f, 0
                if f == "F3a":
                    yield "item", 0
            for n in range(N + max(BACK) + 1):
                b, i = divmod(n, ITEMS2)
                if n:
                    yield "item", n
                if i in BACK and b >= 1:
                    yield BACK[i], b - 1
                if i in FRONT and b + 1 < NB:
                    yield FRONT[i], b + 1

        PARTS = [slice(q0, min(q0 + 512, SPLIT2)) for q0 in range(0, SPLIT2, 512)]
        EARLY = 2
        LATE = 8

        def down_lo(engine):
            return engine.tensor_tensor(down[:, :, 1, :], staged[:, SPLIT2:W2].rearrange("p (e n) -> p e n", e=E2),
                                        down[:, :, 0, :], ALU.subtract)

        with nc.Block() as block:
            @block.sync
            def _(sp):
                sp.dma_start(bias[:, :], bias_dram.partition_broadcast(P)).then_inc(s_land, 16)

            @block.gpsimd
            def _(pool):
                pool.memset(keep_x[:, :], 0.0).then_inc(s_const, 1)
                pool.memset(keep_w[:, :], 0.0).then_inc(s_const, 1)
                pool.memset(sel32, 0.0).then_inc(s_const, 1)
                pool.wait_ge(s_const, 3)
                pool.affine_select(out=keep_x[:, :], in_=keep_x[:, :], compare_op=ALU.is_ge, fill=-1.0,
                                   base=LAT - 1, pattern=[[0, 1]], channel_multiplier=-1).then_inc(s_const, 1)
                pool.affine_select(out=keep_w[:, :], in_=keep_w[:, :], compare_op=ALU.is_ge, fill=-1.0,
                                   base=E2 - 1, pattern=[[0, 1]], channel_multiplier=-1).then_inc(s_const, 1)
                for n in range(2):
                    pool.affine_select(out=sel32, in_=sel32, compare_op=ALU.not_equal, fill=1.0,
                                       base=-n * E2, pattern=[[-1, E2], [0, P]], channel_multiplier=1)\
                        .then_inc(s_const, 1)
                    pool.wait_ge(s_const, 6 + n)
                pool.wait_ge(s_whi, len(PARTS) + 1)
                for cols in PARTS[LATE:]:
                    pool.tensor_tensor(w_lo[:, cols], staged[:, cols], w_hi[:, cols], ALU.subtract).then_inc(s_wlate, 1)
                down_lo(pool).then_inc(s_wlate, 1)
                for what, n in steps():
                    if what == "item" and 2 <= n < N + 2:
                        n -= 2
                        b, i = divmod(n, ITEMS2)
                        pool.wait_ge(s_hh, n + 1)
                        out = s_lo[:, b % 2, :] if i == 0 else h_lo[:, n % RING, :]
                        hi = s_hi[:, b % 2, :] if i == 0 else h_hi[:, n % RING, :]
                        pool.tensor_tensor(out, h[:, n % 4, :], hi, ALU.subtract).then_inc(s_hl, 1)
                    if what == "X0" and n:
                        prep.root(pool, n)
                    if what == "V" and n == NB - 1:
                        next_first.root(pool)
                    if what == "U":
                        addn.root(pool, n)
                    if what == "W" and n < NB - 1:
                        addn.update_x(pool, n)

            @block.scalar
            def _(act):
                act.wait_ge(staged_landed, 16)
                for cols in PARTS:
                    act.activation(w_hi[:, cols], staged[:, cols], ACT.Copy).then_inc(s_whi, 1)
                prep.take_hi(act, 0)
                ins = act.activation(down[:, :, 0, :], staged[:, SPLIT2:W2].rearrange("p (e n) -> p e n", e=E2),
                                     ACT.Copy)
                ins.then_inc(s_whi, 1)
                def h_hi_of(n):
                    b, i = divmod(n, ITEMS2)
                    act.wait_ge(s_h, n + 1)
                    if i == 0 and b >= 2:
                        act.wait_ge(s_v, 2 * (b - 1))
                    if i and n >= RING:
                        d = (n - RING) // ITEMS2 * E2 + (n - RING) % ITEMS2
                        if d:
                            act.wait_ge(s_d, d)
                    out = s_hi[:, b % 2, :] if i == 0 else h_hi[:, n % RING, :]
                    act.activation(out, h[:, n % 4, :], ACT.Copy).then_inc(s_hh, 1)

                def acc_hi(b):
                    act.wait_ge(s_d, (b + 1) * E2)
                    if b:
                        act.wait_ge(s_v, 2 * b)
                    act.activation(a_hi[:, :], acc_bank[:, :], ACT.Copy).then_inc(s_ahi, 1)

                def v_copy(b):
                    for j in range(2):
                        act.wait_ge(s_v, 2 * b + j + 1)
                        if b >= 2:
                            act.wait_ge(addn.s_normed, b - 1)
                        act.activation(v[:, b % 2, 2 * j:2 * j + 2, :], misc[:, :].rearrange("p (t n) -> p t n", t=2),
                                       ACT.Copy).then_inc(s_vc, 1)

                for what, n in steps():
                    if what in ("F1a", "F1b") and n:
                        prep.take_hi(act, n, [int(what == "F1b")])
                    if what == "F2a":
                        act.wait_ge(s_lg, n + 1)
                        if n >= 2:
                            act.wait_ge(s_pt, n - 1)
                        act.activation(probT[:, n % 2, :], misc[0:E2, :], ACT.Sigmoid).then_inc(s_prT, 1)
                        if n == 0:
                            act.wait_ge(s_const, 7)
                            act.activation(sel[:, :, :], sel32, ACT.Copy).then_inc(s_selr, 1)
                    if what == "F2b":
                        act.wait_ge(s_xl, n + 1)
                        if n:
                            act.wait_ge(s_xs, n)
                        act.activation(x_hi[:, :], xl_bank(n)[:, :], ACT.Copy).then_inc(s_xhi, 1)
                    if what == "F4":
                        act.wait_ge(s_wTf, n + 1)
                        if n:
                            act.wait_ge(s_ws, n)
                        act.activation(wT_hi[:, :], misc[0:2 * E2, :], ACT.Copy).then_inc(s_wThi, 1)
                    if what == "item":
                        if n < N:
                            act.wait_ge(s_g, n + 1)
                            if n >= 2:
                                act.wait_ge(s_q, n - 1)
                            act.activation(r[:, n % 2, :], g_bank[n % 2][:, :], ACT.Relu).then_inc(s_r, 1)
                            act.wait_ge(s_r, n + 1)
                            if n >= 2:
                                act.wait_ge(s_qu, n - 1)
                            act.activation(q[:, n % 2, :], r[:, n % 2, :], ACT.Square).then_inc(s_q, 1)
                        if 2 <= n < N + 2:
                            h_hi_of(n - 2)
                        if n >= ITEMS2 and (n - LAG) % ITEMS2 == ITEMS2 - 1:
                            acc_hi((n - LAG) // ITEMS2)
                    if what == "V":
                        v_copy(n)

            @block.vector
            def _(dve):
                tally = Tally(dve)
                prep.take_xn(dve, tally, 0)
                for n, cols in enumerate(PARTS[:LATE]):
                    if n == EARLY:
                        prep.take_lo(dve, tally, 0)
                    dve.wait_ge(s_whi, n + 1)
                    dve.tensor_tensor(w_lo[:, cols], staged[:, cols], w_hi[:, cols], ALU.subtract).then_inc(s_wlo, 1)
                dve.wait_ge(s_const, 7)

                def step(ins):
                    tally(ins, s_step)
                    tally.settle(s_step)

                def choose(b):
                    if b == 0:
                        dve.wait_ge(s_land, 16)
                    dve.wait_ge(s_pt, b + 1)
                    turned = misc[:, 0:TB * E2].rearrange("p (t e) -> p t e", e=E2)
                    dve.tensor_tensor(score[:, :, :], turned, bias[:, :].unsqueeze(1).broadcast_to([P, TB, E2]), ALU.add)\
                       .then_inc(s_step, 1)
                    tally.n[s_step.name] = tally.n.get(s_step.name, 0) + 1
                    tally(dve.tensor_copy(prob[:, :, :], turned), s_pr)
                    tally.settle(s_step)
                    for t in range(TB):
                        ins = dve.max(best[:, t, :], score[:, t, :])
                    step(ins)
                    for t in range(TB):
                        ins = dve.match_replace(rest[:, t, :], best[:, t, :], score[:, t, :], -3e38)
                    step(ins)
                    step(dve.tensor_tensor(rest[:, :, :], rest[:, :, :], score[:, :, :], ALU.not_equal))
                    tally.settle(s_pr)
                    step(dve.tensor_tensor(prob[:, :, :], prob[:, :, :], rest[:, :, :], ALU.mult))

                def weigh(b):
                    step(dve.tensor_reduce(total[:, :, 0], prob[:, :, :], AX.X, ALU.add))
                    step(dve.reciprocal(total[:, :, 0], total[:, :, 0]))
                    for copy in range(2):
                        ins = dve.scalar_tensor_tensor(wt[:, b % 2, :, copy, :], prob[:, :, :], ROUTE_SCALE,
                                                       total[:, :, :].broadcast_to([P, TB, E2]), ALU.mult, ALU.mult)
                    tally(ins, s_wt)

                for what, n in steps():
                    if what == "X0" and n:
                        prep.take_stats(dve, tally, n)
                    if what == "X1" and n:
                        prep.take_xn(dve, tally, n)
                    if what in ("F1a", "F1b") and n:
                        prep.take_lo(dve, tally, n, [int(what == "F1b")])
                    if what == "F2b":
                        dve.wait_ge(s_xhi, n + 1)
                        dve.scalar_tensor_tensor(xs[:, n % 2, :], x_hi[:, :], keep_x[:, 0:1], xl_bank(n)[:, :],
                                                 ALU.mult, ALU.add).then_inc(s_xs, 1)
                    if what == "F3a":
                        choose(n)
                    if what == "F3b":
                        weigh(n)
                    if what == "F4":
                        dve.wait_ge(s_wThi, n + 1)
                        dve.scalar_tensor_tensor(ws[:, n % 2, :], wT_hi[:, :], keep_w[:, 0:1], misc[0:2 * E2, :],
                                                 ALU.mult, ALU.add).then_inc(s_ws, 1)
                    if what == "item" and n < N:
                        b, i = divmod(n, ITEMS2)
                        if n == 0:
                            dve.wait_ge(s_selr, 1)
                        dve.wait_ge(s_u, n + 1)
                        dve.wait_ge(s_q, n + 1)
                        if n >= 4:
                            dve.wait_ge(s_hl, n - 3)
                        if i == 0:
                            dve.tensor_tensor(h[:, n % 4, :], q[:, n % 2, :], u_bank[n % 2][:, :], ALU.mult)\
                               .then_inc(s_h, 1)
                            dve.wait_ge(s_h, n + 1)
                            dve.engine_nop().then_inc(s_qu, 1)
                        else:
                            dve.tensor_tensor(qu[:, n % 2, :], q[:, n % 2, :], u_bank[n % 2][:, :], ALU.mult)\
                               .then_inc(s_qu, 1)
                            dve.wait_ge(s_qu, n + 1)
                            dve.wait_ge(s_b, b * E2 + i)
                            dve.tensor_tensor(h[:, n % 4, :], qu[:, n % 2, :], r_bank[i % 2][:, :], ALU.mult)\
                               .then_inc(s_h, 1)
                    if what == "item" and n >= ITEMS2 and (n - LAG) % ITEMS2 == ITEMS2 - 1:
                        b = (n - LAG) // ITEMS2
                        dve.wait_ge(s_ahi, b + 1)
                        dve.tensor_tensor(a_lo[:, :], acc_bank[:, :], a_hi[:, :], ALU.subtract).then_inc(s_alo, 1)
                    if what == "V" and n == NB - 1:
                        next_first.take_stats(dve)
                    if what == "U":
                        dve.wait_ge(s_vc, 2 * n + 2)
                        addn.take_stats(dve, tally, [v[:, n % 2, t, :] for t in range(TB)])
                    if what == "W":
                        (addn.norm_only if n < NB - 1 else addn.add_normed)(
                            dve, tally, n, [v[:, n % 2, t, :] for t in range(TB)])

            @block.tensor
            def _(pe):
                def both(out, name, stride, i, x0, x1, start, stop, M=P):
                    return three_pass(pe, out, wcol(w_hi, name, i, stride), wcol(w_lo, name, i, stride),
                                      x0, x1, start, stop)

                def values(b):
                    pe.wait_ge(s_alo, b + 1)
                    for j in range(2):
                        if j:
                            pe.wait_ge(s_vc, 2 * b + 1)
                        elif b + 1 < NB:
                            pe.wait_ge(s_ws, b + 2)
                        else:
                            pe.wait_ge(s_vc, 2 * b)
                        for t in range(2 * j, 2 * j + 2):
                            out = misc[:, (t % 2) * HID:(t % 2 + 1) * HID]
                            tk = slice(t * P, (t + 1) * P)
                            three_pass(pe, out, s_hi[:, b % 2, tk], s_lo[:, b % 2, tk],
                                       wcol(w_hi, "shared_down", 0, HID), wcol(w_lo, "shared_down", 0, HID), True, False)
                            ins = three_pass(pe, out, a_hi[:, tk], a_lo[:, tk], wcol(w_hi, "grow", 0, HID),
                                             wcol(w_lo, "grow", 0, HID), False, True)
                        ins.then_inc(s_v, 1)

                for what, n in steps():
                    blk = slice(n * GT, (n + 1) * GT)
                    if what == "F1a":
                        if n == 1:
                            pe.wait_ge(s_ws, 1)
                        elif n:
                            pe.wait_ge(s_vc, 2 * (n - 1))
                    if what in ("F1a", "F1b"):
                        prep.turn(pe, n, [int(what == "F1b")])
                    if what == "F2a":
                        if n == 0:
                            pe.wait_ge(s_wlo, EARLY)
                        pe.wait_ge(prep.s_lo, KH * (n + 1))
                        for k in range(KH):
                            ins = both(misc[0:E2, :], "router", E2, k, xT_hi[:, k, blk], xT_lo[:, k, blk],
                                       k == 0, k == KH - 1)
                        ins.then_inc(s_lg, 1)
                    if what == "F2b":
                        if n:
                            pe.wait_ge(s_prT, n + 1)
                        for k in range(KH):
                            ins = both(xl_bank(n)[:, :], "shrink", P, k, xT_hi[:, k, blk], xT_lo[:, k, blk],
                                       k == 0, k == KH - 1)
                        ins.then_inc(s_xl, 1)
                    if what == "F3a":
                        if n:
                            pe.wait_ge(s_xs, n + 1)
                        pe.wait_ge(s_prT, n + 1)
                        for t in range(TB):
                            ins = pe.transpose(misc[:, t * E2:(t + 1) * E2], probT[:, n % 2, t * P:(t + 1) * P],
                                               ident[0:E2, 0:E2])
                        ins.then_inc(s_pt, 1)
                    if what == "F4":
                        pe.wait_ge(s_wt, n + 1)
                        for t in range(TB):
                            twice = wt[:, n % 2, t, :, :].rearrange("p a e -> p (a e)")
                            ins = pe.transpose(misc[0:2 * E2, t * P:(t + 1) * P], twice, ident[:, :])
                        ins.then_inc(s_wTf, 1)
                    if what == "V":
                        values(n)
                    if what != "item":
                        continue
                    if n < N:
                        b, i = divmod(n, ITEMS2)
                        gb, ub = g_bank[n % 2], u_bank[n % 2]
                        if n == 0:
                            pe.wait_ge(s_wlo, LATE)
                        if i == 1:
                            if b == 0:
                                pe.wait_ge(s_selr, 1)
                                pe.wait_ge(s_wlate, len(PARTS) - LATE + 1)
                            pe.wait_ge(s_ws, b + 1)
                        for which, shared, bk, free, full in (("gate", "shared_gate", gb, s_r, s_g),
                                                              ("up", "shared_up", ub, s_qu, s_u)):
                            if n >= 2:
                                pe.wait_ge(free, n - 1)
                            elif n == 0 and bk is xl_bank(0):
                                pe.wait_ge(s_xs, 1)
                            if i == 0:
                                blk = slice(b * GT, (b + 1) * GT)
                                for k in range(KH):
                                    ins = both(bk[:, :], shared, P, k, xT_hi[:, k, blk], xT_lo[:, k, blk],
                                               k == 0, k == KH - 1)
                            else:
                                pe.matmul(bk[:, :], wcol(w_hi, which, i - 1), xs[:, b % 2, :], start=True, stop=False)
                                ins = pe.matmul(bk[:, :], wcol(w_lo, which, i - 1), xs[:, b % 2, :], start=False, stop=True)
                            ins.then_inc(full, 1)
                        if i:
                            if n - 2 > 0:
                                pe.wait_ge(s_h, n - 1)
                            pe.matmul(r_bank[i % 2][:, :], sel[:, i - 1, :], ws[:, b % 2, :], start=True, stop=True)\
                              .then_inc(s_b, 1)
                    if LAG <= n < N + LAG:
                        b, i = divmod(n - LAG, ITEMS2)
                        if i:
                            pe.wait_ge(s_hl, n - LAG + 1)
                            if i == 1 and b:
                                pe.wait_ge(s_alo, b)
                            dn = down[:, i - 1, :, :].rearrange("p a n -> p (a n)")
                            pe.matmul(acc_bank[:, :], dn, h_hi[:, (n - LAG) % RING, :], start=(i == 1), stop=False,
                                      skip_group_check=True)
                            pe.matmul(acc_bank[:, :], dn, h_lo[:, (n - LAG) % RING, :], start=False, stop=(i == E2),
                                      skip_group_check=True).then_inc(s_d, 1)


H3 = 16
D3 = HID // H3
HG = 4
NG = H3 // HG
REP = 4
SEG = [GT - P * j for j in range(TB)]
OFF = [HG * sum(SEG[:j]) for j in range(TB)]
SCORE_ITEMS = [(j, range(h, h + 1)) for j in (0, 1) for h in range(HG)] + \
              [(j, range(h, HG, 2)) for j in (2, 3) for h in (0, 1)]
SCORES_OF = [4, 8, 10, 12]
BESIDE_SCORES = {1: [("P", 0)], 2: [("T", 0)], 3: [("Q", 0)], 4: [("P", 1)], 5: [("Q", 1)], 6: [("P", 2)],
                 7: [("P", 3)], 8: [("R", 0), ("R", 1)], 9: [("R", 2), ("R", 3)]}
WQK, WV, WO = 0, KH * 2 * HID, KH * 3 * HID
W3 = KH * 4 * HID


def squared_attention(nc, keep, x, xT_hi, xT_lo, ident, half, first, next_first, w_dram, gamma_dram, beta_dram):
    with ExitStack() as ctx:
        c = Core(nc, ctx, keep, "attn1")
        bank = [c.ps(f"bank{i}", [P, 512]) for i in range(8)]
        score_bank, pv_bank = bank[4:7], bank[7]
        N = NB * NG

        def steps():
            yield "A1", 0, 0
            for t in range(TB):
                yield from (("Q", t, 0), ("Q", t, 1), ("W", t, 0), ("U", t, 0))
                if t:
                    yield "N", t - 1, 0
            yield "N", TB - 1, 0
            yield "A3", 0, 0
            yield "A1", 1, 0
            yield from (("R", 0, r) for r in range(4))
            yield from (("Q", TB, 0), ("Q", TB, 1), ("U", TB, 0))
            for n in range(N + 4):
                b, g = divmod(n, NG)
                if g == 1 and b + 2 < NB:
                    yield "A0", b + 2, 0
                if n + TB < NT:
                    yield "N", n + TB, 0
                if g == 2 and b >= 1:
                    yield "O", b - 1, 0
                for i in range(len(SCORE_ITEMS)):
                    if n < N:
                        yield "S", n, i
                    if g == 3 and i == 3 and b + 1 < NB:
                        yield "A3", b + 1, 0
                    for what, r in BESIDE_SCORES.get(i, ()):
                        of, end = {"P": (n - 1, N), "T": (n - 2, N), "R": (n + 1, N), "Q": (n + TB + 1, NT)}[what]
                        if 0 <= of < end:
                            yield what, of, r
                if n + TB + 1 < NT:
                    yield "U", n + TB + 1, 0
                if g == 3 and b >= 1:
                    yield "V", b - 1, 0
                if n + TB < NT:
                    yield "W", n + TB, 0
                if g == 1 and b + 2 < NB:
                    yield "A1", b + 2, 0
                if g in (1, 2) and b >= 2:
                    yield ("Y" if g == 1 else "Z"), b - 2, 0
            yield "Y", NB - 1, 0
            yield "Z", NB - 1, 0

        prep = Prep(c, x, xT_hi, xT_lo, ident, half, first, lambda b, k: shared("xT", b, k),
                    lambda pe, b, k: claim(pe, "xT", b, k))
        addn = AddNorm(c, x, half)
        staged = c.sb("staged", [P, W3])
        w_hi, w_lo = c.sb("w_hi", [P, W3], F32R), c.sb("w_lo", [P, W3], F32R)
        eps = c.sb("eps", [P, 1])
        mean = c.sb("mean", [P, KH * 2 * H3, 1])
        gamma = c.sb("gamma", [P, D3])
        beta = c.sb("beta", [P, D3])
        beta_mean = c.sb("beta_mean", [P, 1])
        beta_row = c.sb("beta_row", [1, 2 * H3, D3])
        beta_hi, beta_lo = c.sb("beta_hi", [1, 2 * H3, D3], F32R), c.sb("beta_lo", [1, 2 * H3, D3], F32R)
        ones = c.sb("ones", [1, P], F32R)
        tri = c.sb("tri", [P, P])
        pick = {(w, part): c.sb(f"pick_{w}_{part}", [P, HG * 2, REP, D3], F32R) for w in "qk" for part in ("hi", "lo")}
        sq = staged[:, 0:4 * HID].rearrange("p (a h d) -> p a h d", a=2, d=D3)
        o = staged[:, 4 * HID:8 * HID].rearrange("p (t g d) -> p t g d", t=TB, g=NG)
        ss = c.sb("ss", [P, 2, 2 * H3, 1])
        qn = c.sb("qn", [P, TB, 2 * HID])
        vp = c.sb("vp", [P, 2, TB, H3, 32])
        c_hi, c_lo = c.sb("c_hi", [P, 4, GT], F32R), c.sb("c_lo", [P, 4, GT], F32R)
        stack = {w: c.sb(f"stack_{w}", [P, 2, 2, GT], F32R) for w in "qk"}
        at = c.sb("at", [P, 2, HG * sum(SEG)])
        copies = at[:, 0, 0:HG * 2 * REP * D3].rearrange("p (h c d) -> p h c d", h=HG * 2, c=REP)
        pvs = c.sb("pvs", [P, GT])
        den = c.sb("den", [P, TB * HG, 1])
        o_hi, o_lo = c.sb("o_hi", [P, KH, GT], F32R), c.sb("o_lo", [P, KH, GT], F32R)

        s_land = c.sem("weights_landed")
        s_const = c.sem("constants")
        s_step = c.sem("weight_step")
        s_whi = c.sem("weights_hi")
        s_wlo = c.sem("weights_lo")
        s_qk = c.sem("qk_full")
        s_vf = c.sem("v_full")
        s_raw = c.sem("qk_copied")
        s_sq = c.sem("squares_done")
        s_ss = c.sem("square_sums")
        s_len = c.sem("qk_length")
        s_rs = c.sem("qk_rstd")
        s_qn = c.sem("qk_normed")
        s_vp = c.sem("v_placed")
        s_cf = c.sem("qk_turned")
        s_chi = c.sem("qk_hi")
        s_clo = c.sem("qk_lo")
        s_rf = c.sem("stack_full")
        s_stack = {"q": c.sem("q_stacked"), "k": c.sem("k_stacked")}
        s_sc = c.sem("scores_full")
        s_at = c.sem("scores_squared")
        s_mask = c.sem("scores_masked")
        s_pv = c.sem("pv_full")
        s_pvc = c.sem("pv_copied")
        s_t = c.sem("pv_turned")
        s_den = c.sem("denominator_step")
        s_o = c.sem("o_ready")
        s_of = c.sem("o_turned")
        s_ohi = c.sem("o_hi")
        s_olo = c.sem("o_lo")
        s_w = c.sem("out_full")
        s_wc = c.sem("out_copied")

        order, released = [], {}
        for what, n, part in steps():
            for key, sem, count in {
                "A1": [(("xT", n, k), prep.s_lo, KH * n + k + 1) for k in range(KH)],
                "Q": [(("qk", n), s_raw, n + 1)] * (part == 0),
                "W": [(("v", n), s_vp, n + 1)],
                "A3": [(("c", n, i), s_clo, 4 * n + i + 1) for i in range(4)],
                "R": [(("r", n, part), s_stack["qk"[part >= 2]], 2 * n + part % 2 + 1)],
                "T": [(("t", n), s_o, n + 1)],
                "O": [(("o", n, k), s_olo, KH * n + k + 1) for k in range(KH)],
                "V": [(("w", n, j), s_wc, 2 * n + j + 1) for j in range(2)],
            }.get(what, []):
                released[key] = sem, count
                order.append(key)
        place = {key: i for i, key in enumerate(order)}

        def shared(*key):
            return bank[place[key] % 4]

        def claim(pe, *key):
            if place[key] >= 4:
                pe.wait_ge(*released[order[place[key] - 4]])
            return shared(*key)

        with nc.Block() as block:
            @block.sync
            def _(sp):
                sp.dma_start(staged[:, :], w_dram).then_inc(s_land, 16)
                sp.dma_start(gamma[:, :], gamma_dram.partition_broadcast(P)).then_inc(s_land, 16)
                sp.dma_start(beta[:, :], beta_dram.partition_broadcast(P)).then_inc(s_land, 16)

            @block.gpsimd
            def _(pool):
                prep.root(pool, 1)
                pool.memset(tri[:, :], 1.0).then_inc(s_const, 1)
                pool.memset(eps[:, :], EPS).then_inc(s_const, 1)
                pool.memset(copies[:, :, :, :], 0.0).then_inc(s_const, 1)
                pool.memset(ones[:, :].bitcast(F32), 1.0).then_inc(s_const, 1)
                pool.memset(vp[:, :, :, :, :], 0.0).then_inc(s_const, 1)
                for m in pick.values():
                    pool.memset(m[:, :, :, :].bitcast(F32), 0.0).then_inc(s_const, 1)
                pool.wait_ge(s_const, 9)
                pool.affine_select(out=tri[:, :], in_=tri[:, :], compare_op=ALU.is_ge, fill=0.0, base=0,
                                   pattern=[[1, P]], channel_multiplier=-1).then_inc(s_const, 1)
                pool.affine_select(out=copies[:, :, :, :], in_=copies[:, :, :, :], compare_op=ALU.not_equal, fill=1.0,
                                   base=0, pattern=[[-D3, HG * 2], [0, REP], [-1, D3]], channel_multiplier=1)\
                    .then_inc(s_const, 1)
                for a in range(2):
                    pool.memset(vp[:, a, :, :, D3:D3 + 1], 1.0).then_inc(s_const, 1)
                for what, n, part in steps():
                    if what == "A0":
                        prep.root(pool, n)
                    if what == "S" and part + 1 in SCORES_OF:
                        j = SCORES_OF.index(part + 1)
                        pool.wait_ge(s_at, len(SCORE_ITEMS) * n + part + 1)
                        diag = at[:, n % 2, OFF[j]:OFF[j] + HG * SEG[j]]\
                            .rearrange("p (h q) -> p h q", h=HG)[:, :, 0:P]
                        pool.tensor_tensor(diag, diag, tri[:, :].unsqueeze(1).broadcast_to([P, HG, P]),
                                           ALU.mult).then_inc(s_mask, 1)
                    if what == "V" and n == NB - 1:
                        next_first.root(pool)
                    if what == "Y":
                        addn.root(pool, n)
                    if what == "Z" and n < NB - 1:
                        addn.update_x(pool, n)

            @block.scalar
            def _(act):
                act.wait_ge(s_land, 48)
                act.activation(w_hi[:, WV:W3], staged[:, WV:W3], ACT.Copy).then_inc(s_whi, 1)
                prep.take_hi(act, 0)
                act.wait_ge(s_step, 6)
                act.activation(w_hi[:, 0:WV], staged[:, 0:WV], ACT.Copy).then_inc(s_whi, 1)
                act.activation(beta_hi[:, :, :], beta_row[:, :, :], ACT.Copy).then_inc(s_whi, 1)
                act.wait_ge(s_const, 13)
                for (w, half_), m in pick.items():
                    a = {("q", "hi"): slice(0, 4, 2), ("q", "lo"): slice(1, 4, 2),
                         ("k", "hi"): slice(0, 2), ("k", "lo"): slice(2, 4)}[w, half_]
                    act.activation(m[:, :, a, :], copies[:, :, a, :], ACT.Copy).then_inc(s_whi, 1)
                for what, n, part in steps():
                    if what == "A1" and n:
                        prep.take_hi(act, n)
                    if what == "Q" and part:
                        act.wait_ge(s_raw, n + 1)
                        if n >= 2:
                            act.wait_ge(s_ss, n - 1)
                        act.activation(sq[:, n % 2, :, :], qn[:, n % TB, :].rearrange("p (h d) -> p h d", d=D3),
                                       ACT.Square, scale=D3 ** -0.5).then_inc(s_sq, 1)
                    if what == "U":
                        act.wait_ge(s_ss, n + 1)
                        act.activation(ss[:, n % 2, :, 0], ss[:, n % 2, :, 0], ACT.Sqrt, bias=eps[:, :]).then_inc(s_len, 1)
                    if what == "W":
                        b, t = divmod(n, TB)
                        act.wait_ge(s_vf, n + 1)
                        if b >= 2:
                            act.wait_ge(s_pv, NG * (b - 1))
                        act.activation(vp[:, b % 2, t, :, 0:D3],
                                       shared("v", n)[:, 0:HID].rearrange("p (h d) -> p h d", d=D3),
                                       ACT.Copy).then_inc(s_vp, 1)
                    if what == "A3":
                        for i in range(4):
                            act.wait_ge(s_cf, 4 * n + i + 1)
                            if n:
                                act.wait_ge(s_rf, 4 * NG * n)
                            act.activation(c_hi[:, i, :], shared("c", n, i)[:, :], ACT.Copy).then_inc(s_chi, 1)
                    if what == "R" and part < 2:
                        act.wait_ge(s_rf, 4 * n + part + 1)
                        if n >= 2:
                            act.wait_ge(s_sc, len(SCORE_ITEMS) * (n - 1))
                        act.activation(stack["q"][:, n % 2, part, :], shared("r", n, part)[:, :], ACT.Copy)\
                           .then_inc(s_stack["q"], 1)
                    if what == "S":
                        if n >= 2:
                            act.wait_ge(s_pv, n - 1)
                        j, heads = SCORE_ITEMS[part]
                        m = len(SCORE_ITEMS) * n + part
                        act.wait_ge(s_sc, m + 1)
                        to = at[:, n % 2, OFF[j]:OFF[j] + HG * SEG[j]].rearrange("p (h q) -> p h q", h=HG)
                        act.activation(to[:, heads.start:heads.stop:heads.step, :],
                                       score_bank[m % 3][:, 0:len(heads) * SEG[j]]
                                       .rearrange("p (h q) -> p h q", h=len(heads)),
                                       ACT.Square, scale=D3 ** -0.5).then_inc(s_at, 1)
                    if what == "O":
                        for k in range(KH):
                            act.wait_ge(s_of, KH * n + k + 1)
                            if n:
                                act.wait_ge(s_w, 2 * n)
                            act.activation(o_hi[:, k, :], shared("o", n, k)[:, :], ACT.Copy).then_inc(s_ohi, 1)
                    if what == "V":
                        for j in range(2):
                            act.wait_ge(s_w, 2 * n + j + 1)
                            if n:
                                act.wait_ge(addn.s_x, n)
                            act.activation(addn.normed[:, 2 * j:2 * j + 2, :],
                                           shared("w", n, j)[:, :].rearrange("p (t n) -> p t n", t=2), ACT.Copy)\
                               .then_inc(s_wc, 1)

            @block.vector
            def _(dve):
                tally = Tally(dve)
                prep.take_xn(dve, tally, 0)
                prep.take_stats(dve, tally, 1)
                dve.wait_ge(s_land, 48)

                def step(ins):
                    tally(ins, s_step)
                    tally.settle(s_step)

                wqk = staged[:, 0:WV].rearrange("p (g d) -> p g d", d=D3)
                step(dve.tensor_tensor(wqk, wqk, gamma[:, :].unsqueeze(1).broadcast_to([P, KH * 2 * H3, D3]), ALU.mult))
                dve.tensor_reduce(mean[:, :, 0], wqk, AX.X, ALU.add).then_inc(s_step, 1)
                tally.n[s_step.name] += 1
                step(dve.tensor_reduce(beta_mean[:, :], beta[:, :], AX.X, ALU.add))
                step(dve.scalar_tensor_tensor(wqk, mean[:, :, :].broadcast_to([P, KH * 2 * H3, D3]), -1.0 / D3, wqk,
                                              ALU.mult, ALU.add))
                step(dve.scalar_tensor_tensor(beta[:, :], beta_mean[:, :].broadcast_to([P, D3]), -1.0 / D3, beta[:, :],
                                              ALU.mult, ALU.add))
                step(dve.tensor_copy(beta_row[:, :, :], beta[0:1, :].unsqueeze(1).broadcast_to([1, 2 * H3, D3])))
                dve.wait_ge(s_whi, 1)
                dve.tensor_tensor(w_lo[:, WV:W3], staged[:, WV:W3], w_hi[:, WV:W3], ALU.subtract).then_inc(s_wlo, 1)
                prep.take_lo(dve, tally, 0)
                dve.wait_ge(s_whi, 2)
                dve.tensor_tensor(w_lo[:, 0:WV], staged[:, 0:WV], w_hi[:, 0:WV], ALU.subtract).then_inc(s_wlo, 1)
                dve.wait_ge(s_whi, 3)
                dve.tensor_tensor(beta_lo[:, :, :], beta_row[:, :, :], beta_hi[:, :, :], ALU.subtract).then_inc(s_wlo, 1)
                for what, n, part in steps():
                    if what == "A0":
                        prep.take_stats(dve, tally, n)
                    if what == "A1" and n:
                        prep.take_xn(dve, tally, n)
                        prep.take_lo(dve, tally, n)
                    if what == "Q" and part:
                        b, t = divmod(n, TB)
                        dve.wait_ge(s_qk, n + 1)
                        if b:
                            dve.wait_ge(s_cf, 4 * b)
                        dve.tensor_copy(qn[:, t, :], shared("qk", n)[:, :]).then_inc(s_raw, 1)
                    if what == "U":
                        dve.wait_ge(s_sq, n + 1)
                        if n >= 2:
                            dve.wait_ge(s_qn, n - 1)
                        dve.tensor_reduce(ss[:, n % 2, :, 0], sq[:, n % 2, :, :], AX.X, ALU.add).then_inc(s_ss, 1)
                    if what == "N":
                        dve.wait_ge(s_len, n + 1)
                        dve.reciprocal(ss[:, n % 2, :, 0], ss[:, n % 2, :, 0]).then_inc(s_rs, 1)
                        dve.wait_ge(s_rs, n + 1)
                        dve.wait_ge(s_raw, n + 1)
                        qk = qn[:, n % TB, :].rearrange("p (h d) -> p h d", d=D3)
                        dve.tensor_tensor(qk, qk, ss[:, n % 2, :, :].broadcast_to([P, 2 * H3, D3]), ALU.mult)\
                           .then_inc(s_qn, 1)
                    if what == "A3":
                        for i in range(4):
                            dve.wait_ge(s_chi, 4 * n + i + 1)
                            dve.tensor_tensor(c_lo[:, i, :], shared("c", n, i)[:, :], c_hi[:, i, :], ALU.subtract)\
                               .then_inc(s_clo, 1)
                    if what == "R" and part >= 2:
                        dve.wait_ge(s_rf, 4 * n + part + 1)
                        if n >= 2:
                            dve.wait_ge(s_sc, len(SCORE_ITEMS) * (n - 1))
                        dve.tensor_copy(stack["k"][:, n % 2, part - 2, :], shared("r", n, part)[:, :])\
                           .then_inc(s_stack["k"], 1)
                    if what == "P" and part == TB - 1:
                        dve.wait_ge(s_pv, n + 1)
                        if n:
                            dve.wait_ge(s_t, n)
                        dve.tensor_copy(pvs[:, :], pv_bank[:, :]).then_inc(s_pvc, 1)
                    if what == "T":
                        b, g = divmod(n, NG)
                        turned = shared("t", n)[:, :].rearrange("p (a d) -> p a d", d=32)
                        dve.wait_ge(s_t, n + 1)
                        if n:
                            dve.wait_ge(s_o, n)
                        tally(dve.tensor_scalar(den[:, :, :], turned[:, :, D3:D3 + 1], EPS, None, ALU.add), s_den)
                        tally.settle(s_den)
                        tally(dve.reciprocal(den[:, :, :], den[:, :, :]), s_den)
                        tally.settle(s_den)
                        if g == 0 and b:
                            dve.wait_ge(s_of, KH * b)
                        dve.tensor_tensor(o[:, :, g, :].rearrange("p t (h d) -> p t h d", d=D3),
                                          turned[:, :, 0:D3].rearrange("p (t h) d -> p t h d", t=TB),
                                          den[:, :, :].rearrange("p (t h) d -> p t h d", t=TB).broadcast_to([P, TB, HG, D3]),
                                          ALU.mult).then_inc(s_o, 1)
                    if what == "O":
                        for k in range(KH):
                            dve.wait_ge(s_ohi, KH * n + k + 1)
                            dve.tensor_tensor(o_lo[:, k, :], shared("o", n, k)[:, :], o_hi[:, k, :], ALU.subtract)\
                               .then_inc(s_olo, 1)
                    if what == "V" and n == NB - 1:
                        next_first.take_stats(dve)
                    if what == "Y":
                        dve.wait_ge(s_wc, 2 * n + 2)
                        addn.take_stats(dve, tally, [addn.normed[:, t, :] for t in range(TB)])
                    if what == "Z":
                        (addn.norm_only if n < NB - 1 else addn.add_normed)(
                            dve, tally, n, [addn.normed[:, t, :] for t in range(TB)])

            @block.tensor
            def _(pe):
                for what, n, part in steps():
                    if what == "A1":
                        prep.turn(pe, n)
                    if what == "Q":
                        if n == 0 and part == 0:
                            pe.wait_ge(s_wlo, 3)
                            pe.wait_ge(s_whi, 3)
                            pe.wait_ge(s_const, 4)
                        pe.wait_ge(prep.s_lo, KH * (n // TB + 1))
                        tok = slice(n * P, (n + 1) * P)
                        out = (shared if part else partial(claim, pe))("qk", n)[:, :]
                        k = part
                        cols = slice(WQK + k * 2 * HID, WQK + (k + 1) * 2 * HID)
                        three_pass(pe, out, xT_hi[:, k, tok], xT_lo[:, k, tok], w_hi[:, cols], w_lo[:, cols],
                                   k == 0, False)
                        if part:
                            pe.matmul(out, ones[:, :], beta_hi[:, :, :].rearrange("p h d -> p (h d)"), start=False,
                                      stop=False, skip_group_check=True)
                            pe.matmul(out, ones[:, :], beta_lo[:, :, :].rearrange("p h d -> p (h d)"), start=False,
                                      stop=True, skip_group_check=True).then_inc(s_qk, 1)
                    if what == "W":
                        tok = slice(n * P, (n + 1) * P)
                        out = claim(pe, "v", n)[:, 0:HID]
                        for k in range(KH):
                            cols = slice(WV + k * HID, WV + (k + 1) * HID)
                            ins = three_pass(pe, out, xT_hi[:, k, tok], xT_lo[:, k, tok], w_hi[:, cols],
                                             w_lo[:, cols], k == 0, k == KH - 1)
                        ins.then_inc(s_vf, 1)
                    if what == "A3":
                        pe.wait_ge(s_qn, TB * (n + 1))
                        for i in range(4):
                            out = claim(pe, "c", n, i)
                            for t in range(TB):
                                ins = pe.transpose(out[:, t * P:(t + 1) * P], qn[:, t, i * P:(i + 1) * P], ident[:, :])
                            ins.then_inc(s_cf, 1)
                    if what == "R":
                        b, g = divmod(n, NG)
                        if n == 0:
                            pe.wait_ge(s_whi, 7)
                        if g == 0:
                            pe.wait_ge(s_clo, 4 * (b + 1))
                        out = claim(pe, "r", n, part)[:, :]
                        pair = 2 * g + part % 2
                        rows = part // 2 * 2 + pair // 4
                        for half_, src in (("hi", c_hi), ("lo", c_lo)):
                            m = pick["qk"[part // 2], half_][:, 2 * (pair % 4):2 * (pair % 4) + 2, :, :]
                            ins = pe.matmul(out, m.rearrange("p h c d -> p (h c d)"), src[:, rows, :],
                                            start=(half_ == "hi"), stop=(half_ == "lo"))
                        ins.then_inc(s_rf, 1)
                    if what == "S":
                        if part == 0:
                            pe.wait_ge(s_stack["q"], 2 * (n + 1))
                            pe.wait_ge(s_stack["k"], 2 * (n + 1))
                        j, heads = SCORE_ITEMS[part]
                        m = len(SCORE_ITEMS) * n + part
                        if m >= 3:
                            pe.wait_ge(s_at, m - 2)
                        for at_, h in enumerate(heads):
                            row = slice(64 * (h % 2), 64 * (h % 2) + 64)
                            ins = pe.matmul(score_bank[m % 3][:, at_ * SEG[j]:(at_ + 1) * SEG[j]],
                                            stack["k"][row, n % 2, h // 2, j * P:(j + 1) * P],
                                            stack["q"][row, n % 2, h // 2, j * P:GT], start=True, stop=True)
                        ins.then_inc(s_sc, 1)
                    if what == "P":
                        b, g = divmod(n, NG)
                        j = part
                        if j == 0:
                            if n:
                                pe.wait_ge(s_pvc, n)
                            if g == 0:
                                pe.wait_ge(s_vp, TB * (b + 1))
                        pe.wait_ge(s_mask, TB * n + j + 1)
                        for h in range(HG):
                            a = OFF[j] + h * SEG[j]
                            ins = pe.matmul(pv_bank[32 * h:32 * h + 32, j * P:GT], vp[:, b % 2, j, HG * g + h, :],
                                            at[:, n % 2, a:a + SEG[j]], start=(j == 0), stop=(j == TB - 1),
                                            skip_group_check=True)
                        if j == TB - 1:
                            ins.then_inc(s_pv, 1)
                    if what == "T":
                        pe.wait_ge(s_pvc, n + 1)
                        out = claim(pe, "t", n)
                        for t in range(TB):
                            ins = pe.transpose(out[:, t * P:(t + 1) * P], pvs[:, t * P:(t + 1) * P], ident[:, :])
                        ins.then_inc(s_t, 1)
                    if what == "O":
                        pe.wait_ge(s_o, NG * (n + 1))
                        for k in range(KH):
                            out = claim(pe, "o", n, k)
                            for t in range(TB):
                                ins = pe.transpose(out[:, t * P:(t + 1) * P],
                                                   o[:, t, 2 * k:2 * k + 2, :].rearrange("p g d -> p (g d)"), ident[:, :])
                            ins.then_inc(s_of, 1)
                    if what == "V":
                        pe.wait_ge(s_olo, KH * (n + 1))
                        for j in range(2):
                            out = claim(pe, "w", n, j)
                            for t in range(2 * j, 2 * j + 2):
                                tok = slice(t * P, (t + 1) * P)
                                for k in range(KH):
                                    cols = slice(WO + k * HID, WO + (k + 1) * HID)
                                    ins = three_pass(pe, out[:, (t % 2) * HID:(t % 2 + 1) * HID], o_hi[:, k, tok],
                                                     o_lo[:, k, tok], w_hi[:, cols], w_lo[:, cols], k == 0, k == KH - 1)
                            ins.then_inc(s_w, 1)


H1 = 8
D1 = 64
INNER = H1 * D1
KI = INNER // P
STATE = 128
CHUNK = P
BCD = 2 * STATE + H1
PROJ = 2 * INNER + BCD
W1 = KH * PROJ + KI * HID


def mamba(nc, keep, x, x_dram, ident, half, next_first, w_dram, rows_dram, cols_dram, next_w, next_w_dram, next_landed):
    with ExitStack() as ctx:
        c = Core(nc, ctx, keep, "attn0")
        bank = [c.ps(f"bank{i}", [P, 512]) for i in range(8)]
        addn = AddNorm(c, x, half)
        staged = c.sb("staged", [P, W1])
        w_hi, w_lo = c.sb("w_hi", [P, W1], F32R), c.sb("w_lo", [P, W1], F32R)
        rows = c.sb("rows", [P, 3, H1])
        cols = c.sb("cols", [P, 2 + 2 * KH])
        bc_w = c.sb("bc_w", [P, 1])
        le = c.sb("le", [P, P])
        gt32 = c.sb("gt32", [P, P])
        gt = c.sb("gt", [P, P], F32R)
        ones = c.sb("ones", [P, P])
        stats = c.sb("stats", [P, TB, 6])
        moments = c.sb("moments", [P, TB, 2])
        rstd = c.sb("rstd", [P, 3, TB])
        a = c.sb("a", [P, 2, TB, HID])
        un = c.sb("un", [P, TB, HID])
        uT = c.sb("uT", [P, KH, GT])
        u_hi, u_lo = c.sb("u_hi", [P, KH, GT], F32R), c.sb("u_lo", [P, KH, GT], F32R)
        zs = c.sb("zs", [P, 2, TB, INNER])
        xs = c.sb("xs", [P, 2, TB, INNER])
        junk = c.sb("junk", [P, STATE])
        norm = c.sb("norm", [P, 2, TB, 2])
        bt, ct = c.sb("bt", [P, 2, TB, STATE]), c.sb("ct", [P, TB, STATE])
        bT, cT = c.sb("bT", [P, 2, GT]), c.sb("cT", [P, 2, GT])
        dt = c.sb("dt", [P, 2, TB, H1])
        dts = c.sb("dts", [P, 6, TB, H1])
        da = c.sb("da", [P, TB, H1])
        da_hi, da_lo = c.sb("da_hi", [P, 2, TB, H1], F32R), c.sb("da_lo", [P, 2, TB, H1], F32R)
        expo = c.sb("expo", [P, 3, TB, H1])
        decay = c.sb("decay", [P, 2, 3, TB, H1])
        seg_hi, seg_lo = c.sb("seg_hi", [P, H1, P], F32R), c.sb("seg_lo", [P, H1, P], F32R)
        el = c.sb("el", [P, H1, P])
        gm = c.sb("gm", [P, 2, P])
        m = c.sb("m", [P, H1, P])
        xd = c.sb("xd", [P, 2, INNER])
        xdec = c.sb("xdec", [P, 2, INNER])
        st = c.sb("st", [P, 2, INNER])
        y_hi, y_lo = c.sb("y_hi", [P, KI, P], F32R), c.sb("y_lo", [P, KI, P], F32R)
        v = c.sb("v", [P, TB, HID])
        th, sd, t1, t2, y1, y2 = (staged[:, i * INNER:(i + 1) * INNER] for i in range(6))

        sems = {n: c.sem(n) for n in (
            "landed", "const", "w_hi", "w_lo", "w_lo_pool", "stats", "moments", "r_step", "rstd", "a", "un", "u_turned", "uT", "u_hi",
            "u_lo", "z_full", "x_full", "bcd_full", "tanh", "zs", "xs", "bc_sum", "bc_eps", "dt_raw", "bc_rstd", "bc", "bc_raw", "bT_full",
            "cT_full", "bT", "cT", "sp_act", "sp_dve", "da", "cum_full", "expo", "decay", "seg_rhs", "seg_full",
            "seg_exp", "g_full", "gm", "m", "xd", "xdec", "yo_full", "st_full", "yd_full", "sd", "t1", "t2", "st",
            "y1", "y2", "y_turned", "y_hi", "y_lo", "v_full", "v", "r_step_dve")}

        x_landed = [c.sem(f"x_landed{b}") for b in range(NB)]
        w_landed = [c.sem(f"w_landed{i}") for i in range(3)]
        ident_ready = c.sem("ident_ready")

        def steps():
            yield "A0", 0, 0
            yield "A1", 0, 0
            yield "AA", 0, 0
            yield "A0", 1, 0
            for t in range(TB):
                yield "A2", 0, t
            yield "A3", 0, 0
            yield "AS", 1, 0
            yield "A1", 1, 0
            yield "AA", 1, 0
            for what in ("G", "A4", "X", "B1"):
                yield what, 0, 0
            beside = {0: (("A2", 0),), 1: (("AA", 0), ("A2", 1), ("A2", 2)), 2: (("A2", 3), ("A3", 0)), 3: ()}
            for i in range(NT + 1):
                b, t = divmod(i, TB)
                if i < NT:
                    yield "SD", b, t
                if i + 1 < NT:
                    yield "G", *divmod(i + 1, TB)
                if t == 2 and b + 2 < NB:
                    yield "A0", b + 2, 0
                if t == 1 and b:
                    yield "DR", b - 1, 0
                if i < NT:
                    yield "B2", b, t
                if t == 1 and b:
                    yield "D2", b - 1, 0
                if t == 3 and b + 1 < NB:
                    yield "A4", b + 1, 0
                if i + 1 < NT:
                    yield "X", *divmod(i + 1, TB)
                if i:
                    yield "C1", *divmod(i - 1, TB)
                if i + 1 < NT:
                    yield "B1", *divmod(i + 1, TB)
                if b + 1 < NB:
                    for what, t_ in beside[t]:
                        if what != "AA" or b:
                            yield what, b + 1, t_
                if t == 3 and b + 2 < NB:
                    yield "AS", b + 2, 0
                    yield "A1", b + 2, 0
                if i:
                    yield "C2", *divmod(i - 1, TB)
                if i and t == 0:
                    yield "D1", b - 1, 0
            yield "DR", NB - 1, 0
            yield "D2", NB - 1, 0

        order, released = [], {}
        for what, b, t in steps():
            i = TB * b + t
            for key, sem, count in {
                "A1": [(("u", b, k), "uT", KH * b + k + 1) for k in range(KH)],
                "A2": [(("z", i), "zs", i + 1), (("x", i), "xs", i + 1), (("bcd", i), "dt_raw", i + 1)],
                "A4": [(("bT", b), "bT", b + 1), (("cT", b), "cT", b + 1), (("cum", b), "expo", 2 * b + 1)],
                "B1": [(("seg", i, j), "seg_exp", 2 * i + j + 1) for j in range(2)] + [(("g", i), "gm", i + 1)],
                "B2": [(("yo", i), "t1", 3 * b + t)] * (t > 0) + [(("st", i), "st", 3 * b + t + 1)] * (t < TB - 1)
                      + [(("yd", i), "t2", i + 1)],
                "C1": [(("y", i), "y_lo", i + 1)],
                "C2": [(("v", i), "v", i + 1)],
            }.get(what, ()):
                released[key] = sems[sem], count
                order.append(key)
        place = {key: n for n, key in enumerate(order)}

        def bank_of(*key):
            return bank[place[key] % 8]

        def claim(pe, *key):
            if place[key] >= 8:
                pe.wait_ge(*released[order[place[key] - 8]])
            return bank_of(*key)

        PARTS = W1 // 600
        POOL_PARTS = 2

        def split_weights(engine, n, done):
            cols_ = slice(n * 600, (n + 1) * 600)
            engine.wait_ge(sems["w_hi"], n + 1)
            engine.tensor_tensor(w_lo[:, cols_], staged[:, cols_], w_hi[:, cols_], ALU.subtract).then_inc(done, 1)

        def heads(ap):
            return ap.rearrange("p (h d) -> p h d", h=H1)

        with nc.Block() as block:
            @block.sync
            def _(sp):
                def load_x(b):
                    tiles = slice(b * TB, (b + 1) * TB)
                    sp.dma_start(x[:, tiles, :], x_dram[:, tiles, :]).then_inc(x_landed[b], 16)

                load_x(0)
                for i in range(3):
                    part = slice(i * W1 // 3, (i + 1) * W1 // 3)
                    sp.dma_start(staged[:, part], w_dram[:, part]).then_inc(w_landed[i], 16)
                sp.dma_start(rows[:, :, :], rows_dram.partition_broadcast(P)).then_inc(sems["landed"], 16)
                sp.dma_start(cols[:, :], cols_dram).then_inc(sems["landed"], 16)
                for b in range(1, NB):
                    load_x(b)
                sp.dma_start(next_w[:, :], next_w_dram).then_inc(next_landed, 16)

            @block.gpsimd
            def _(pool):
                pool.memset(half[:, :], -0.5).then_inc(ident_ready, 1)
                pool.memset(ident[:, :], 0.0).then_inc(ident_ready, 1)
                pool.wait_ge(ident_ready, 2)
                pool.affine_select(out=ident[:, :], in_=ident[:, :], compare_op=ALU.not_equal, fill=1.0, base=0,
                                   pattern=[[-1, P]], channel_multiplier=1).then_inc(ident_ready, 1)
                pool.memset(le[:, :], 1.0).then_inc(sems["const"], 1)
                pool.memset(gt32[:, :], 1.0).then_inc(sems["const"], 1)
                pool.memset(ones[:, :], 1.0).then_inc(sems["const"], 1)
                pool.wait_ge(sems["const"], 3)
                pool.affine_select(out=le[:, :], in_=le[:, :], compare_op=ALU.is_ge, fill=0.0, base=0,
                                   pattern=[[1, P]], channel_multiplier=-1).then_inc(sems["const"], 1)
                pool.affine_select(out=gt32[:, :], in_=gt32[:, :], compare_op=ALU.is_gt, fill=0.0, base=0,
                                   pattern=[[-1, P]], channel_multiplier=1).then_inc(sems["const"], 1)
                for what, b, t in steps():
                    i = TB * b + t
                    if what == "A1" and b == 0:
                        for n in range(PARTS - POOL_PARTS, PARTS):
                            split_weights(pool, n, sems["w_lo_pool"])
                    if what == "A0":
                        pool.wait_ge(sems["moments"], b + 1)
                        if b:
                            pool.wait_ge(sems["un"], b)
                        var = moments[:, :, 1]
                        r_step, n = sems["r_step"], 6 * b
                        pool.tensor_scalar(rstd[:, 0, :], var, EPS, None, ALU.add).then_inc(r_step, 1)
                        pool.wait_ge(r_step, n + 1)
                        pool.tensor_tensor(rstd[:, 0, :], rstd[:, 0, :], half[:, 0:TB], ALU.pow).then_inc(r_step, 1)
                        pool.wait_ge(r_step, n + 2)
                        pool.tensor_tensor(rstd[:, 1, :], rstd[:, 0, :], rstd[:, 0, :], ALU.mult).then_inc(r_step, 1)
                        pool.wait_ge(r_step, n + 3)
                        pool.tensor_tensor(rstd[:, 1, :], rstd[:, 1, :], var, ALU.mult).then_inc(r_step, 1)
                        pool.wait_ge(r_step, n + 4)
                        inverse_root(pool, rstd[:, 1, :], half[:, 0:TB], r_step, n + 5, r_step)
                        pool.wait_ge(r_step, n + 6)
                        pool.tensor_tensor(rstd[:, 2, :], rstd[:, 1, :], rstd[:, 0, :], ALU.mult)\
                            .then_inc(sems["rstd"], 1)
                    if what == "A3":
                        pool.wait_ge(sems["bc_raw"], TB * (b + 1))
                        inverse_root(pool, norm[:, b % 2].rearrange("p t j -> p (t j)"), half[:, 0:2 * TB],
                                     sems["bc_eps"], b + 1, sems["bc_rstd"], EPS * STATE)
                    if what == "SD" and 0 < t < TB - 1:
                        n = 3 * b + t
                        pool.wait_ge(sems["st"], n)
                        pool.tensor_tensor(heads(sd), heads(st[:, (n - 1) % 2, :]),
                                                  decay[:, b % 2, 1, t, :].unsqueeze(2).broadcast_to([P, H1, D1]),
                                                  ALU.mult).then_inc(sems["sd"], 1)
                    if what == "G":
                        pool.wait_ge(sems["da"], 2 * b + 2)
                        if i:
                            pool.wait_ge(sems["seg_full"], 2 * i)
                        for out, d in ((seg_hi, da_hi), (seg_lo, da_lo)):
                            for q in range(2):
                                hs = slice(4 * q, 4 * q + 4)
                                pool.tensor_tensor(out[:, hs, :], d[:, b % 2, t, hs].unsqueeze(2).broadcast_to([P, 4, P]),
                                                   le[:, :].unsqueeze(1).broadcast_to([P, 4, P]), ALU.mult)\
                                    .then_inc(sems["seg_rhs"], 1)
                        pool.wait_ge(sems["xs"], i + 1)
                        if i >= 2:
                            pool.wait_ge(sems["t2"], i - 1)
                        pool.tensor_tensor(heads(xd[:, i % 2, :]), heads(xs[:, b % 2, t, :]),
                                                  rows[:, 0, :].unsqueeze(2).broadcast_to([P, H1, D1]),
                                                  ALU.mult).then_inc(sems["xd"], 1)
                    if what == "X":
                        if t < TB - 1:
                            pool.wait_ge(sems["decay"], b + 1)
                            if 3 * b + t >= 2:
                                pool.wait_ge(sems["st_full"], 3 * b + t - 1)
                            pool.tensor_tensor(heads(xdec[:, (3 * b + t) % 2, :]), heads(xs[:, b % 2, t, :]),
                                                      decay[:, b % 2, 2, t, :].unsqueeze(2).broadcast_to([P, H1, D1]),
                                                      ALU.mult).then_inc(sems["xdec"], 1)
                    if what == "B2":
                        pool.wait_ge(sems["y1"], i + 1)
                        if i:
                            pool.wait_ge(sems["y_turned"], i)
                        pool.tensor_tensor(y2, y1, zs[:, b % 2, t, :], ALU.mult).then_inc(sems["y2"], 1)
                    if what == "DR":
                        if b == NB - 1:
                            next_first.root(pool)
                        addn.root(pool, b)

            @block.scalar
            def _(act):
                for q0 in range(0, W1, 600):
                    act.wait_ge(w_landed[q0 // 1200], 16)
                    act.activation(w_hi[:, q0:q0 + 600], staged[:, q0:q0 + 600], ACT.Copy).then_inc(sems["w_hi"], 1)
                act.wait_ge(sems["landed"], 32)
                act.activation(rows[:, 2, :], rows[:, 2, :], ACT.Exp).then_inc(sems["sp_act"], 1)
                act.wait_ge(sems["const"], 5)
                act.activation(gt[:, :], gt32[:, :], ACT.Copy).then_inc(sems["const"], 1)
                for what, b, t in steps():
                    i = TB * b + t
                    if what == "A1":
                        for k in range(KH):
                            act.wait_ge(sems["u_turned"], KH * b + k + 1)
                            if b:
                                act.wait_ge(sems["u_lo"], KH * (b - 1) + k + 1)
                            act.activation(uT[:, k, :], bank_of("u", b, k)[:, :], ACT.Identity,
                                           scale=cols[:, 2 + k:3 + k], bias=cols[:, 2 + KH + k:3 + KH + k])\
                               .then_inc(sems["uT"], 1)
                            act.wait_ge(sems["uT"], KH * b + k + 1)
                            if b:
                                act.wait_ge(sems["bcd_full"], TB * b)
                            act.activation(u_hi[:, k, :], uT[:, k, :], ACT.Copy).then_inc(sems["u_hi"], 1)
                    if what == "A2":
                        act.wait_ge(sems["z_full"], i + 1)
                        if i:
                            act.wait_ge(sems["zs"], i)
                        act.activation(th, bank_of("z", i)[:, :], ACT.Tanh, scale=0.5).then_inc(sems["tanh"], 1)
                        act.wait_ge(sems["x_full"], i + 1)
                        if b >= 2:
                            act.wait_ge(sems["yd_full"], TB * (b - 1))
                            act.wait_ge(sems["xd"], TB * (b - 1))
                        act.activation(xs[:, b % 2, t, :], bank_of("x", i)[:, :], ACT.Copy).then_inc(sems["xs"], 1)
                        act.wait_ge(sems["bcd_full"], i + 1)
                        if b >= 2 and t == 0:
                            act.wait_ge(sems["bc"], b - 1)
                        for j in range(2):
                            if 2 * i + j:
                                act.wait_ge(sems["bc_sum"], 2 * i + j)
                            act.activation(junk[:, :], bank_of("bcd", i)[:, j * STATE:(j + 1) * STATE], ACT.Square,
                                           accum_out=norm[:, b % 2, t, j:j + 1]).then_inc(sems["bc_sum"], 1)
                        if b >= 2 and t == 0:
                            act.wait_ge(sems["st_full"], 3 * (b - 1))
                        if b and t == 0:
                            act.wait_ge(sems["cT_full"], b)
                        act.activation(bt[:, b % 2, t, :], bank_of("bcd", i)[:, 0:STATE], ACT.Copy)
                        act.activation(ct[:, t, :], bank_of("bcd", i)[:, STATE:2 * STATE], ACT.Copy)\
                           .then_inc(sems["bc_raw"], 1)
                    if what == "A3":
                        n = 3 * b
                        act.wait_ge(sems["dt_raw"], TB * (b + 1))
                        if b:
                            act.wait_ge(sems["sp_dve"], 5 * b)
                        act.activation(dts[:, 0], dt[:, b % 2], ACT.Abs).then_inc(sems["sp_act"], 1)
                        act.wait_ge(sems["sp_act"], n + 2)
                        act.activation(dts[:, 1], dts[:, 0], ACT.Exp, scale=-1.0).then_inc(sems["sp_act"], 1)
                        act.wait_ge(sems["sp_dve"], 5 * b + 1)
                        act.activation(dts[:, 3], dts[:, 2], ACT.Ln).then_inc(sems["sp_act"], 1)
                    if what == "A4":
                        for w, scale in (("bT", 1.0), ("cT", bc_w[:, 0:1])):
                            act.wait_ge(sems[w + "_full"], b + 1)
                            if b >= 2:
                                act.wait_ge(sems["g_full"], TB * (b - 1))
                            act.activation((bT if w == "bT" else cT)[:, b % 2, :], bank_of(w, b)[:, :], ACT.Copy,
                                           scale=scale).then_inc(sems[w], 1)
                        act.wait_ge(sems["expo"], 2 * b + 2)
                        if b >= 2:
                            act.wait_ge(sems["t1"], 3 * (b - 1))
                            act.wait_ge(sems["xdec"], 3 * (b - 1))
                            act.wait_ge(sems["sd"], 2 * (b - 1))
                        act.activation(decay[:, b % 2], expo[:, :, :, :], ACT.Exp).then_inc(sems["decay"], 1)
                    if what == "B1":
                        for j in range(2):
                            act.wait_ge(sems["seg_full"], 2 * i + j + 1)
                            if i and j == 0:
                                act.wait_ge(sems["m"], i)
                            act.activation(el[:, 4 * j:4 * j + 4, :],
                                           bank_of("seg", i, j)[:, :].rearrange("p (h l) -> p h l", h=4),
                                           ACT.Exp).then_inc(sems["seg_exp"], 1)
                    if what == "C1":
                        act.wait_ge(sems["y_turned"], i + 1)
                        if i:
                            act.wait_ge(sems["v_full"], i)
                        act.activation(y_hi[:, :, :], bank_of("y", i)[:, :].rearrange("p (k l) -> p k l", k=KI),
                                       ACT.Copy, scale=0.5).then_inc(sems["y_hi"], 1)

            @block.vector
            def _(dve):
                tally = Tally(dve)

                def measure(b):
                    dve.wait_ge(x_landed[b], 16)
                    for t in range(TB):
                        ins = dve.bn_stats(stats[:, t, :], x[:, b * TB + t, :])
                    tally(ins, sems["stats"])
                    tally.settle(sems["stats"])
                    for t in range(TB):
                        ins = dve.bn_aggr(moments[:, t, :], stats[:, t, :])
                    tally(ins, sems["moments"])

                def scale(b):
                    dve.wait_ge(sems["rstd"], b + 1)
                    if b:
                        dve.wait_ge(sems["u_turned"], KH * b)
                    for t in range(TB):
                        ins = dve.tensor_scalar(un[:, t, :], x[:, b * TB + t, :], moments[:, t, 0:1],
                                                rstd[:, 2, t:t + 1], ALU.subtract, ALU.mult)
                    tally(ins, sems["un"])

                def scale_a(b):
                    for t in range(TB):
                        ins = dve.tensor_scalar(a[:, b % 2, t, :], x[:, b * TB + t, :], moments[:, t, 0:1],
                                                rstd[:, 0, t:t + 1], ALU.subtract, ALU.mult)
                    tally(ins, sems["a"])

                measure(0)
                for n in range(PARTS - POOL_PARTS):
                    if n == 2:
                        scale(0)
                    split_weights(dve, n, sems["w_lo"])
                dve.wait_ge(sems["landed"], 32)
                dve.scalar_tensor_tensor(bc_w[:, :], cols[:, 0:1], float(STATE), cols[:, 1:2], ALU.mult, ALU.mult)\
                   .then_inc(sems["w_lo"], 1)
                dve.wait_ge(sems["const"], 6)
                for what, b, t in steps():
                    i = TB * b + t
                    if what == "A0" and b:
                        measure(b)
                    if what == "AA":
                        scale_a(b)
                    if what == "AS":
                        scale(b)
                    if what == "A1":
                        for k in range(KH):
                            dve.wait_ge(sems["u_hi"], KH * b + k + 1)
                            dve.tensor_tensor(u_lo[:, k, :], uT[:, k, :], u_hi[:, k, :], ALU.subtract)\
                               .then_inc(sems["u_lo"], 1)
                    if what == "A2":
                        dve.wait_ge(sems["tanh"], i + 1)
                        if b >= 2:
                            dve.wait_ge(sems["y2"], TB * (b - 1))
                        dve.scalar_tensor_tensor(zs[:, b % 2, t, :], th, 1.0, bank_of("z", i)[:, :], ALU.add, ALU.mult)\
                           .then_inc(sems["zs"], 1)
                        dve.wait_ge(sems["bc_raw"], i + 1)
                        dve.tensor_tensor(dt[:, b % 2, t, :], bank_of("bcd", i)[:, 2 * STATE:BCD], rows[:, 1, :], ALU.add)\
                           .then_inc(sems["dt_raw"], 1)
                    if what == "A3":
                        sp = sems["sp_dve"]
                        e, u, ln, d, eq = dts[:, 1], dts[:, 2], dts[:, 3], dts[:, 4], dts[:, 5]
                        dve.wait_ge(sems["sp_act"], 3 * b + 3)
                        tally(dve.tensor_scalar(u, e, 1.0, None, ALU.add), sp)
                        tally.settle(sp)
                        dve.tensor_scalar(d, u, -1.0, None, ALU.add)
                        tally(dve.tensor_scalar(eq, u, 1.0, None, ALU.is_equal), sp)
                        tally.settle(sp)
                        tally(dve.tensor_tensor(d, d, eq, ALU.add), sp)
                        dve.wait_ge(sems["bc_rstd"], b + 1)
                        for t_ in range(TB):
                            for j, rows_ in enumerate((bt[:, b % 2, t_, :], ct[:, t_, :])):
                                ins = dve.tensor_scalar(rows_, rows_, norm[:, b % 2, t_, j:j + 1], None, ALU.mult)
                        ins.then_inc(sems["bc"], 1)
                        dve.wait_ge(sems["sp_act"], 3 * b + 4)
                        tally.settle(sp)
                        tally(dve.reciprocal(d, d), sp)
                        dve.tensor_tensor(ln, ln, eq, ALU.add)
                        tally.settle(sp)
                        chain = sems["r_step_dve"]
                        def step(ins):
                            tally(ins, chain)
                            tally.settle(chain)
                        step(dve.tensor_tensor(d, d, e, ALU.mult))
                        step(dve.tensor_tensor(d, d, ln, ALU.mult))
                        step(dve.scalar_tensor_tensor(d, dt[:, b % 2], 0.0, d, ALU.max, ALU.add))
                        if b:
                            dve.wait_ge(sems["cum_full"], b)
                        step(dve.scalar_tensor_tensor(da[:, :, :], d, -1.0,
                                                      rows[:, 2, :].unsqueeze(1).broadcast_to([P, TB, H1]),
                                                      ALU.mult, ALU.mult))
                        tally(dve.engine_nop(), sp)
                        if b >= 2:
                            dve.wait_ge(sems["seg_rhs"], 4 * TB * (b - 1))
                        tally(dve.tensor_copy(da_hi[:, b % 2], da[:, :, :]), sems["da"])
                        tally.settle(sems["da"])
                        tally(dve.tensor_tensor(da_lo[:, b % 2], da[:, :, :], da_hi[:, b % 2], ALU.subtract), sems["da"])
                    if what == "A4":
                        dve.wait_ge(sems["cum_full"], b + 1)
                        if b:
                            dve.wait_ge(sems["decay"], b)
                        tally(dve.tensor_copy(expo[:, 0:2], bank_of("cum", b)[:, 0:2 * TB * H1]
                                              .rearrange("p (a t h) -> p a t h", a=2, t=TB)), sems["expo"])
                        tally.settle(sems["expo"])
                        tally(dve.tensor_tensor(expo[:, 2], expo[:, 1], expo[:, 0], ALU.subtract), sems["expo"])
                    if what == "B1":
                        dve.wait_ge(sems["g_full"], i + 1)
                        dve.tensor_tensor(gm[:, i % 2, :], bank_of("g", i)[:, 0:P], le[:, :], ALU.mult).then_inc(sems["gm"], 1)
                        dve.wait_ge(sems["gm"], i + 1)
                        dve.wait_ge(sems["seg_exp"], 2 * i + 2)
                        if i:
                            dve.wait_ge(sems["yd_full"], i)
                        dve.tensor_tensor(m[:, :, :], el[:, :, :], gm[:, i % 2, :].unsqueeze(1).broadcast_to([P, H1, P]),
                                          ALU.mult).then_inc(sems["m"], 1)
                    if what == "B2":
                        if t:
                            dve.wait_ge(sems["yo_full"], 3 * b + t)
                            if i:
                                dve.wait_ge(sems["y1"], i)
                            dve.tensor_tensor(heads(t1), heads(bank_of("yo", i)[:, :]),
                                              decay[:, b % 2, 0, t, :].unsqueeze(2).broadcast_to([P, H1, D1]), ALU.mult)\
                               .then_inc(sems["t1"], 1)
                        if t < TB - 1:
                            n = 3 * b + t
                            dve.wait_ge(sems["st_full"], n + 1)
                            if n >= 2:
                                dve.wait_ge(sems["yo_full"], n - 1)
                            if t:
                                dve.wait_ge(sems["sd"], 2 * b + t)
                                dve.tensor_tensor(st[:, n % 2, :], bank_of("st", i)[:, :], sd, ALU.add)\
                                   .then_inc(sems["st"], 1)
                            else:
                                dve.tensor_copy(st[:, n % 2, :], bank_of("st", i)[:, :]).then_inc(sems["st"], 1)
                        dve.wait_ge(sems["yd_full"], i + 1)
                        dve.wait_ge(sems["xd"], i + 1)
                        if i:
                            dve.wait_ge(sems["y2"], i)
                            dve.wait_ge(sems["y1"], i)
                        dve.tensor_tensor(t2 if t else y1, bank_of("yd", i)[:, :], xd[:, i % 2, :], ALU.add)\
                           .then_inc(sems["t2"], 1)
                        dve.wait_ge(sems["t2"], i + 1)
                        if t:
                            dve.wait_ge(sems["t1"], 3 * b + t)
                            dve.tensor_tensor(y1, t1, t2, ALU.add).then_inc(sems["y1"], 1)
                        else:
                            dve.engine_nop().then_inc(sems["y1"], 1)
                    if what == "C1":
                        dve.wait_ge(sems["y_hi"], i + 1)
                        dve.scalar_tensor_tensor(y_lo[:, :, :].rearrange("p k l -> p (k l)"), bank_of("y", i)[:, :], 0.5,
                                                 y_hi[:, :, :].rearrange("p k l -> p (k l)"), ALU.mult, ALU.subtract)\
                           .then_inc(sems["y_lo"], 1)
                    if what == "C2" and i == NT - 1:
                        next_first.take_stats(dve)
                    if what == "C2":
                        dve.wait_ge(sems["v_full"], i + 1)
                        dve.wait_ge(sems["a"], b + 1)
                        tally(dve.tensor_tensor(v[:, t, :], bank_of("v", i)[:, 0:HID], a[:, b % 2, t, :], ALU.add), sems["v"])
                    if what == "D1":
                        tally.settle(sems["v"])
                        addn.take_stats(dve, tally, [v[:, t_, :] for t_ in range(TB)])
                    if what == "D2":
                        addn.add_normed(dve, tally, b, [v[:, t_, :] for t_ in range(TB)])

            @block.tensor
            def _(pe):
                for what, b, t in steps():
                    i = TB * b + t
                    tok = slice(t * P, (t + 1) * P)
                    if what == "A1":
                        pe.wait_ge(sems["un"], b + 1)
                        if b == 0:
                            pe.wait_ge(ident_ready, 3)
                        for k in range(KH):
                            out = claim(pe, "u", b, k)
                            for t_ in range(TB):
                                ins = pe.transpose(out[:, t_ * P:(t_ + 1) * P], un[:, t_, k * P:(k + 1) * P], ident[:, :])
                            ins.then_inc(sems["u_turned"], 1)
                    if what == "A2":
                        if i == 0:
                            pe.wait_ge(sems["w_lo"], PARTS - POOL_PARTS)
                            pe.wait_ge(sems["w_lo_pool"], POOL_PARTS)
                        if t == 0:
                            pe.wait_ge(sems["u_lo"], KH * (b + 1))
                        for name, c0, n in (("z", 0, INNER), ("x", INNER, INNER), ("bcd", 2 * INNER, BCD)):
                            out = claim(pe, name, i)[:, 0:n]
                            for k in range(KH):
                                wc = slice(k * PROJ + c0, k * PROJ + c0 + n)
                                ins = three_pass(pe, out, u_hi[:, k, tok], u_lo[:, k, tok], w_hi[:, wc], w_lo[:, wc],
                                                 k == 0, k == KH - 1)
                            ins.then_inc(sems[name + "_full"], 1)
                    if what == "A4":
                        pe.wait_ge(sems["bc"], b + 1)
                        for name in ("bT", "cT"):
                            out = claim(pe, name, b)
                            for t_ in range(TB):
                                src = bt[:, b % 2, t_, :] if name == "bT" else ct[:, t_, :]
                                ins = pe.transpose(out[:, t_ * P:(t_ + 1) * P], src, ident[:, :])
                            ins.then_inc(sems[name + "_full"], 1)
                        pe.wait_ge(sems["da"], 2 * b + 1)
                        out = claim(pe, "cum", b)
                        rhs = da[:, :, :].rearrange("p t h -> p (t h)")
                        pe.matmul(out[:, 0:TB * H1], le[:, :], rhs, start=True, stop=True)
                        pe.matmul(out[:, TB * H1:2 * TB * H1], ones[:, :], rhs, start=True, stop=True)\
                          .then_inc(sems["cum_full"], 1)
                    if what == "B1":
                        for j in range(2):
                            out = claim(pe, "seg", i, j)[:, :]
                            hs = slice(4 * j, 4 * j + 4)
                            if i == 0:
                                pe.wait_ge(sems["const"], 6)
                            pe.wait_ge(sems["seg_rhs"], 4 * i + 4)
                            pe.matmul(out, gt[:, :], seg_hi[:, hs, :].rearrange("p h l -> p (h l)"), start=True, stop=False)
                            pe.matmul(out, gt[:, :], seg_lo[:, hs, :].rearrange("p h l -> p (h l)"), start=False, stop=True)\
                              .then_inc(sems["seg_full"], 1)
                        if t == 0:
                            pe.wait_ge(sems["cT"], b + 1)
                            pe.wait_ge(sems["bT"], b + 1)
                        out = claim(pe, "g", i)
                        pe.matmul(out[:, 0:P], bT[:, b % 2, tok], cT[:, b % 2, tok], start=True, stop=True)\
                          .then_inc(sems["g_full"], 1)
                    if what == "B2":
                        if t:
                            out = claim(pe, "yo", i)
                            pe.wait_ge(sems["st"], 3 * b + t)
                            pe.matmul(out[:, :], cT[:, b % 2, tok], st[:, (3 * b + t - 1) % 2, :], start=True, stop=True)\
                              .then_inc(sems["yo_full"], 1)
                        if t < TB - 1:
                            out = claim(pe, "st", i)
                            pe.wait_ge(sems["xdec"], 3 * b + t + 1)
                            pe.matmul(out[:, :], bt[:, b % 2, t, :], xdec[:, (3 * b + t) % 2, :], start=True, stop=True)\
                              .then_inc(sems["st_full"], 1)
                        out = claim(pe, "yd", i)
                        pe.wait_ge(sems["m"], i + 1)
                        for h in range(H1):
                            ins = pe.matmul(out[:, h * D1:(h + 1) * D1], m[:, h, :], xs[:, b % 2, t, h * D1:(h + 1) * D1],
                                            start=True, stop=True)
                        ins.then_inc(sems["yd_full"], 1)
                    if what == "C1":
                        pe.wait_ge(sems["y2"], i + 1)
                        out = claim(pe, "y", i)
                        for k in range(KI):
                            ins = pe.transpose(out[:, k * P:(k + 1) * P], y2[:, k * P:(k + 1) * P], ident[:, :])
                        ins.then_inc(sems["y_turned"], 1)
                    if what == "C2":
                        out = claim(pe, "v", i)[:, 0:HID]
                        pe.wait_ge(sems["y_lo"], i + 1)
                        for k in range(KI):
                            wc = slice(KH * PROJ + k * HID, KH * PROJ + (k + 1) * HID)
                            ins = three_pass(pe, out, y_hi[:, k, :], y_lo[:, k, :], w_hi[:, wc], w_lo[:, wc],
                                             k == 0, k == KI - 1)
                        ins.then_inc(sems["v_full"], 1)


def two_layers(nc, x_dram, w1_dram, rows1_dram, cols1_dram, w2_dram, bias2_dram, w3_dram, gamma_dram, beta_dram,
               router_dram, w4_dram, out_dram):
    with ExitStack() as whole:
        c = Core(nc, whole, [], "all")
        keep = []
        x = c.sb("x", [P, NT, HID])
        ident = c.sb("ident", [P, P])
        half = c.sb("half", [P, P])
        w2_landed = c.sem("w2_landed")

        firsts = [FirstGroup(Core(nc, whole, [], f"first{n}"), x, half) for n in (2, 3, 4)]

        def with_xT(tag, layer, *args):
            with ExitStack() as ctx:
                here = Core(nc, ctx, keep, tag)
                layer(nc, keep, x, *(here.sb(name, [P, KH, TOK], F32R) for name in ("xT_hi", "xT_lo")), ident, half, *args)

        with ExitStack() as two:
            w2 = Core(nc, two, keep, "w2").sb("staged", [P, W2])
            mamba(nc, keep, x, x_dram, ident, half, firsts[0], w1_dram, rows1_dram, cols1_dram, w2, w2_dram, w2_landed)
            nc.clear_and_free_semaphores(keep)
            nc.all_engine_barrier()
            keep = []
            with_xT("two", routed_ffn, firsts[0], firsts[1], w2, w2_landed, bias2_dram)
        with_xT("three", squared_attention, firsts[1], firsts[2], w3_dram, gamma_dram, beta_dram)
        with_xT("four", top_p_ffn, firsts[2], w4_dram, router_dram, out_dram)


def kernel(**inputs):
    import numpy as np
    import concourse.bacc as bacc
    from concourse.bass_utils import run_bass_kernel_spmd

    w = {name: np.asarray(a) for name, a in inputs.items()}

    def by_input(m):
        return m.T.reshape(-1, P, m.shape[0]).transpose(1, 0, 2).reshape(P, -1)

    def by_tile(v):
        return v.reshape(-1, P).T

    def twice(m):
        return np.concatenate([m, m], 0)

    def experts(m):
        return m.transpose(2, 0, 1).reshape(m.shape[2], -1)

    a0, f0, a1, f1 = ({name[len(p):]: v for name, v in w.items() if name.startswith(p)}
                      for p in ("L0_attn_", "L0_ffn_", "L1_attn_", "L1_ffn_"))
    laid = {
        "x": a0["u"].reshape(NT, P, HID).transpose(1, 0, 2),
        "w1": np.concatenate([by_input(a0["in_proj_w"]), by_input(a0["out_proj_w"])], 1),
        "rows1": np.stack([a0["D"], a0["dt_bias"], a0["A_log"]]),
        "cols1": np.concatenate([by_tile(a0[n]) for n in ("bnorm_w", "cnorm_w", "ln_w", "ln_b")], 1),
        "w2": np.concatenate([
            by_input(f0["Wg"]), by_input(twice(f0["Wdown"])), by_input(f0["sw1"]), by_input(f0["swg"]),
            by_input(f0["sw2"]), twice(experts(f0["rw1"])), twice(experts(f0["rwg"])), twice(f0["Wup"].T),
            experts(f0["rw2"])], 1),
        "bias2": f0["biases"],
        "w3": np.concatenate([by_input(np.concatenate([a1["Wq"], a1["Wk"]], 0)), by_input(a1["Wv"]),
                              by_input(a1["Wo"])], 1),
        "gamma": a1["gamma"],
        "beta": a1["beta"],
        "router": f1["router_w"].T.reshape(KH, P, E4).transpose(1, 0, 2),
        "w4": np.stack([np.concatenate([by_input(f1[n][e]) for n in ("gate_w", "up_w", "down_w")], 1)
                        for e in range(E4)]),
    }
    nc = bacc.Bacc("TRN2", target_bir_lowering=False, num_devices=1)
    arrays, args = {}, []
    for name, a in laid.items():
        arrays[name] = np.ascontiguousarray(a)
        args.append(nc.dram_tensor(name, a.shape, mybir.dt.from_np(a.dtype), kind="ExternalInput").ap())
    args.append(nc.dram_tensor("out", [P, NT, HID], F32, kind="ExternalOutput").ap())
    two_layers(nc, *args)
    r = run_bass_kernel_spmd(nc, [arrays], core_ids=[0])
    return r.results[0]["out"].transpose(1, 0, 2).reshape(a0["u"].shape)
```
